# Optimizing a Trainium2 kernel written in Bass

```python
import numpy as np
import jax
import jax.numpy as jnp

def _softmax(x, axis=-1):
    return jax.nn.softmax(x, axis=axis)

def _gelu(x):
    return jax.nn.gelu(x, approximate=True)

def _silu(x):
    return jax.nn.silu(x)

def _sigmoid(x):
    return jax.nn.sigmoid(x)

def _layernorm(x, axis=-1, eps=1e-05):
    m = jnp.mean(x, axis=axis, keepdims=True)
    v = jnp.var(x, axis=axis, keepdims=True)
    return (x - m) / jnp.sqrt(v + eps)

def _scatter_add(tgt, idx, src, axis=0):
    return tgt.at[idx].add(src)

def _segment_sum(src, seg, n):
    return jax.ops.segment_sum(src, seg, n)
kernel_name = 'mk_rec_standalone_d1_rec_r8_c4a14f'

def setup_inputs(seed: int=0):
    np.random.seed(seed)
    _w = jnp.asarray

    def _rec_inputs():
        import jax
        import jax.numpy as jnp
        _rk = jax.random.key(seed)
        r_edge_index = jnp.stack([jax.random.randint(jax.random.fold_in(jax.random.fold_in(_rk, 1), 0), (125000,), 0, 62500, jnp.int32), jax.random.randint(jax.random.fold_in(jax.random.fold_in(_rk, 1), 1), (125000,), 1, 499999, jnp.int32)], axis=0)
        r_cate_features = jax.random.randint(jax.random.fold_in(_rk, 2), (5, 125000), 0, 1250, jnp.int32)
        return (r_edge_index, r_cate_features)
    r_edge_index, r_cate_features = _rec_inputs()

    def _L0_rec_setup():
        import jax, jax.numpy as jnp
        import numpy as np
        N = 62500
        D = 64
        L = 3
        E = 125000
        OFF = 1250
        CATE = 5
        CONT = 8
        EPS = 1e-05

        def layer_norm(x, g, b):
            m = x.mean(-1, keepdims=True)
            v = ((x - m) ** 2).mean(-1, keepdims=True)
            return (x - m) * jax.lax.rsqrt(v + EPS) * g + b
        key = jax.random.key(seed)
        ks = jax.random.split(key, 12)
        edge_index = jax.random.randint(ks[0], (2, E), 0, N)
        cate_features = jax.random.randint(ks[1], (CATE, E), 0, OFF)
        cont_features = jax.random.normal(ks[2], (CONT, E), dtype=jnp.float32)
        s = float(np.sqrt(6.0 / (N + D)))
        node_emb = jax.random.uniform(ks[3], (N, D), minval=-s, maxval=s, dtype=jnp.float32)
        cate_table = (jax.random.normal(ks[4], (OFF, D), dtype=jnp.float32) * 0.02).at[0].set(0.0)
        Wc = jax.random.normal(ks[5], (D * CATE, D), dtype=jnp.float32) * 0.02
        bc = jnp.zeros((D,), jnp.float32)
        ln1_g = jnp.ones((D,), jnp.float32)
        ln1_b = jnp.zeros((D,), jnp.float32)
        bn_g = jnp.ones((CONT,), jnp.float32)
        bn_b = jnp.zeros((CONT,), jnp.float32)
        Wq = jax.random.normal(ks[6], (CONT, D), dtype=jnp.float32) * 0.1
        bq = jnp.zeros((D,), jnp.float32)
        ln2_g = jnp.ones((D,), jnp.float32)
        ln2_b = jnp.zeros((D,), jnp.float32)
        Wm = jax.random.normal(ks[7], (2 * D, D), dtype=jnp.float32) * 0.05
        bm = jnp.zeros((D,), jnp.float32)
        ln3_g = jnp.ones((D,), jnp.float32)
        ln3_b = jnp.zeros((D,), jnp.float32)
        Wf = jax.random.normal(ks[8], (3 * D, 1), dtype=jnp.float32) * 0.05
        bf = jnp.zeros((1,), jnp.float32)
        return dict(edge_index=edge_index, cate_features=cate_features, cont_features=cont_features, node_emb=node_emb, cate_table=cate_table, Wc=Wc, bc=bc, ln1_g=ln1_g, ln1_b=ln1_b, bn_g=bn_g, bn_b=bn_b, Wq=Wq, bq=bq, ln2_g=ln2_g, ln2_b=ln2_b, Wm=Wm, bm=bm, ln3_g=ln3_g, ln3_b=ln3_b, Wf=Wf, bf=bf)
    _L0_rec_all = _L0_rec_setup()
    _L0_rec_in = {k: v for k, v in _L0_rec_all.items() if k in ('cont_features', 'node_emb', 'cate_table', 'Wc', 'bc', 'ln1_g', 'ln1_b', 'bn_g', 'bn_b', 'Wq', 'bq', 'ln2_g', 'ln2_b', 'Wm', 'bm', 'ln3_g', 'ln3_b', 'Wf', 'bf')}
    del _L0_rec_all
    return {'r_edge_index': r_edge_index, 'r_cate_features': r_cate_features, 'L0_rec_cont_features': _L0_rec_in['cont_features'], 'L0_rec_node_emb': _L0_rec_in['node_emb'], 'L0_rec_cate_table': _L0_rec_in['cate_table'], 'L0_rec_Wc': _L0_rec_in['Wc'], 'L0_rec_bc': _L0_rec_in['bc'], 'L0_rec_ln1_g': _L0_rec_in['ln1_g'], 'L0_rec_ln1_b': _L0_rec_in['ln1_b'], 'L0_rec_bn_g': _L0_rec_in['bn_g'], 'L0_rec_bn_b': _L0_rec_in['bn_b'], 'L0_rec_Wq': _L0_rec_in['Wq'], 'L0_rec_bq': _L0_rec_in['bq'], 'L0_rec_ln2_g': _L0_rec_in['ln2_g'], 'L0_rec_ln2_b': _L0_rec_in['ln2_b'], 'L0_rec_Wm': _L0_rec_in['Wm'], 'L0_rec_bm': _L0_rec_in['bm'], 'L0_rec_ln3_g': _L0_rec_in['ln3_g'], 'L0_rec_ln3_b': _L0_rec_in['ln3_b'], 'L0_rec_Wf': _L0_rec_in['Wf'], 'L0_rec_bf': _L0_rec_in['bf']}

def reference(r_edge_index, r_cate_features, L0_rec_cont_features, L0_rec_node_emb, L0_rec_cate_table, L0_rec_Wc, L0_rec_bc, L0_rec_ln1_g, L0_rec_ln1_b, L0_rec_bn_g, L0_rec_bn_b, L0_rec_Wq, L0_rec_bq, L0_rec_ln2_g, L0_rec_ln2_b, L0_rec_Wm, L0_rec_bm, L0_rec_ln3_g, L0_rec_ln3_b, L0_rec_Wf, L0_rec_bf):
    import jax
    import jax.numpy as jnp

    def _L0_rec_ref(edge_index, cate_features, cont_features, node_emb, cate_table, Wc, bc, ln1_g, ln1_b, bn_g, bn_b, Wq, bq, ln2_g, ln2_b, Wm, bm, ln3_g, ln3_b, Wf, bf):
        import jax, jax.numpy as jnp
        import numpy as np
        N = 62500
        D = 64
        L = 3
        E = 125000
        OFF = 1250
        CATE = 5
        CONT = 8
        EPS = 1e-05

        def layer_norm(x, g, b):
            m = x.mean(-1, keepdims=True)
            v = ((x - m) ** 2).mean(-1, keepdims=True)
            return (x - m) * jax.lax.rsqrt(v + EPS) * g + b
        src, dst = (edge_index[0], edge_index[1])
        deg = jax.ops.segment_sum(jnp.ones((E,), node_emb.dtype), dst, num_segments=N)
        dis = jnp.where(deg > 0, jax.lax.rsqrt(jnp.maximum(deg, 1.0)), 0.0)
        norm = dis[src] * dis[dst]
        alpha = 1.0 / (L + 1)
        x = node_emb
        out = x * alpha
        for _ in range(L):
            x = jax.ops.segment_sum(x[src] * norm[:, None], dst, num_segments=N)
            out = out + x * alpha
        out_src = out[src]
        out_dst = out[dst]
        cf = cate_features.T
        ce = cate_table[cf] * (cf != 0)[..., None].astype(node_emb.dtype)
        cate_emb = layer_norm(ce.reshape(E, CATE * D) @ Wc + bc, ln1_g, ln1_b)
        cx = cont_features.T
        mu = cx.mean(0)
        var = ((cx - mu) ** 2).mean(0)
        cxn = (cx - mu) * jax.lax.rsqrt(var + EPS) * bn_g + bn_b
        cont_emb = layer_norm(cxn @ Wq + bq, ln2_g, ln2_b)
        seq = jnp.concatenate([cate_emb, cont_emb], axis=1)
        seq = layer_norm(jax.nn.relu(seq) @ Wm + bm, ln3_g, ln3_b)
        h = jnp.concatenate([out_src, out_dst, seq], axis=1)
        return (h @ Wf + bf).reshape(-1)
    y = _L0_rec_ref(r_edge_index, r_cate_features, L0_rec_cont_features, L0_rec_node_emb, L0_rec_cate_table, L0_rec_Wc, L0_rec_bc, L0_rec_ln1_g, L0_rec_ln1_b, L0_rec_bn_g, L0_rec_bn_b, L0_rec_Wq, L0_rec_bq, L0_rec_ln2_g, L0_rec_ln2_b, L0_rec_Wm, L0_rec_bm, L0_rec_ln3_g, L0_rec_ln3_b, L0_rec_Wf, L0_rec_bf)
    return y

_drawn_inputs = setup_inputs


def setup_inputs(seed=0):
    import zlib

    import numpy as np

    out = dict(_drawn_inputs(seed))
    spreads = {'L0_rec_bc': (0.0, 0.1),
     'L0_rec_ln1_g': (1.0, 0.2),
     'L0_rec_ln1_b': (0.0, 0.497),
     'L0_rec_bn_g': (1.0, 0.2),
     'L0_rec_bn_b': (0.0, 0.1),
     'L0_rec_bq': (0.0, 0.1),
     'L0_rec_ln2_g': (1.0, 0.2),
     'L0_rec_ln2_b': (0.0, 0.1),
     'L0_rec_bm': (0.0, 0.1),
     'L0_rec_ln3_g': (1.0, 0.2),
     'L0_rec_ln3_b': (0.0, 0.321)}
    factors = {'L0_rec_node_emb': 56.898}
    for name, (base, spread) in spreads.items():
        noise = np.random.default_rng([zlib.crc32(name.encode()), seed]).standard_normal(out[name].shape)
        drawn = base * np.exp(spread * noise) if base else spread * noise
        out[name] = jnp.asarray(drawn.astype(out[name].dtype))
    for name, factor in factors.items():
        out[name] = (out[name] * factor).astype(out[name].dtype)
    return out
```

```python
import concourse.bass as bass
from concourse import mybir
from contextlib import ExitStack
import numpy as np

N = 62500
D = 64
E = 125000
OFF = 1250
CATE = 5
CONT = 8
LAYERS = 3
EPS = 1e-5
P = 125
COLS = E // P
HI = N // P
HALF = COLS // 2
TOP = 8
ROUND = 2 * TOP
ROUNDS_MAX = -(-HALF // TOP)
LISTW = (ROUNDS_MAX + 1) * ROUND
FILL_SRC = -float(2 ** 25)
FILL_DST = -float(2 ** 25) + 65534.0
SB = 1000
TILES = SB // P
NSB = E // SB
BLK = 500
NB = SB // BLK
KT = OFF // P
NKT = CATE * KT
RING = 10
TB = BLK // P


def rec_kernel(nc, src_e, dst_e, cate, cont, node_emb, tableT, Wc, bc, ln1_g, ln1_b, bn_g, bn_b,
               Wq, bq, ln2_g, ln2_b, Wm, bm, ln3_g, ln3_b, Wf, bf, y):
    f32, bf16, f16, i32 = mybir.dt.float32, mybir.dt.bfloat16, mybir.dt.float16, mybir.dt.int32
    ALU, ACT, AX = mybir.AluOpType, mybir.ActivationFunctionType, mybir.AxisListType
    ds = bass.ds
    RMAX = bass.bass_isa.ReduceOp.max
    ctx = ExitStack()
    with ctx:
        def sb(name, shape, dt=f32):
            return ctx.enter_context(nc.sbuf_tensor(name, shape, dt))

        def sem(name):
            return ctx.enter_context(nc.semaphore(name))

        cate16_d = nc.dram_tensor("cate16_d", [NSB, CATE * SB], f16, kind="Internal").ap()
        cxn_d = nc.dram_tensor("cxn_d", [NSB, CONT * SB], f32, kind="Internal").ap()
        u_d = [nc.dram_tensor(f"u{l}_d", [N, 6], f32, kind="Internal").ap() for l in range(LAYERS)]
        out_d = nc.dram_tensor("out_d", [N, 2], f32, kind="Internal").ap()

        def views(area):
            at = [0]

            def take(shape, dt=f32):
                n = int(np.prod(shape[1:]))
                size = 2 if dt in (f16, bf16) else 4
                words = -(-n * size // 4)
                v = area[0:shape[0], at[0]:at[0] + words]
                at[0] += words
                assert at[0] <= area.shape[1], (at[0], area.shape)
                if dt != f32:
                    v = v.bitcast(dt)
                if len(shape) > 2:
                    names = "abcd"[:len(shape) - 1]
                    v = v.rearrange(f"p ({' '.join(names)}) -> p {' '.join(names)}", **dict(zip(names, shape[1:])))
                return v
            return take

        wide = sb("wide", [128, 16200])
        take = views(wide)
        cont_f = take([P, CONT, SB])
        cate_i = take([P, CATE * SB], i32)
        cate_h = take([P, CATE * SB], f16)
        take = views(wide)
        tabT = take([D, OFF])
        Tf = take([P, KT, CATE, D])
        take = views(wide)
        onehot = [take([P, SB], f16) for _ in range(RING)]
        cate_b = [take([P, CATE, SB], f16) for _ in range(2)]
        cx = [take([CONT, SB]) for _ in range(2)]
        lo_part = [take([D, BLK]) for _ in range(NB)]
        SD = [take([128, BLK]) for _ in range(NB)]
        R = [take([128, BLK]) for _ in range(NB)]
        sortmem = sb("sortmem", [P, 2 * LISTW])
        keys = views(sortmem)([P, 2, 2, HALF])
        packed_i = views(sortmem)([P, 2, LISTW], i32)
        listmem = sb("listmem", [P, 3 * LISTW])
        take = views(listmem)
        col_key = take([P, 2, HALF])
        valid = take([P, COLS], i32)
        dst_f = take([P, COLS])
        tri = views(listmem)([P, 3, LISTW], i32)
        NCH = 25
        CH = HI // NCH
        nodemem = sb("nodemem", [P, 4 * CH * D])
        take = views(nodemem)
        nchunk = [take([P, CH, D]) for _ in range(2)]
        nprod = [take([P, CH, D]) for _ in range(2)]
        utab = views(nodemem)([P, HI, 6])

        ends = sb("ends", [P, 2, COLS], i32)
        top8 = sb("top8", [P, 2, 2, TOP])
        packed = sb("packed", [P, 2, LISTW])
        cnt = sb("cnt", [P, 2])
        cmax = sb("cmax", [P, 1])
        call = sb("call", [P, 1])
        nround = sb("nround", [P, 2], i32)
        slot = [sb(f"slot{h}", [P, 3, TOP], i32) for h in range(2)]
        gath = [sb(f"gath{h}", [P, TOP, 6]) for h in range(2)]
        oh_hi = [sb(f"oh_hi{k}", [P, HI], bf16) for k in range(2)]
        oh_lo = [sb(f"oh_lo{k}", [P, 6, P], bf16) for k in range(2)]
        iota_i = sb("iota_i", [P, 2, HALF], i32)
        iota16 = sb("iota16", [P, HI], f16)
        zero_l = sb("zero_l", [P, P], bf16)
        xnode = sb("xnode", [P, 2, HI])
        outn = sb("outn", [P, 2, HI])
        dis = sb("dis", [P, HI])
        degm = sb("degm", [P, HI])
        un = sb("un", [P, 2, HI])
        xl = sb("xl", [P, 2, HI])
        part_b = sb("part_b", [P, 2, HI], bf16)
        wf_s = sb("wf_s", [P, 3, D])

        bstat = sb("bstat", [P, 4, CONT])
        sqj = sb("sqj", [P, SB])
        bnp = sb("bnp", [P, 2, CONT])
        onesm = sb("onesm", [P, P])
        row_i = sb("row_i", [P, KT], i32)
        row_f = sb("row_f", [P, KT])
        wc = sb("wc", [D, CATE, D])
        wsum = sb("wsum", [128, 8])
        T16 = sb("T16", [P, KT, CATE, 2 * D], f16)
        bcb = sb("bcb", [P, D])
        tmax = sb("tmax", [128, 2])
        sc_i = sb("sc_i", [128, 2], i32)
        wq = sb("wq", [CONT, D])
        bqr = sb("bqr", [1, D])
        one1 = sb("one1", [1, 1])
        bqc = sb("bqc", [128, 1])
        g12 = sb("g12", [128, 1])
        b12 = sb("b12", [128, 1])
        eps = sb("eps", [128, 1])
        wm = sb("wm", [128, D + 1])
        gw = sb("gw", [128, D])
        wtmp = sb("wtmp", [128, D])
        brow = sb("brow", [P, D + 1])
        v3 = sb("v3", [128, 4, D])
        bfb = sb("bfb", [P, 1])
        k0 = sb("k0", [P, 2])
        blockones = sb("blockones", [128, 128])
        X = [[sb(f"X{q}{b}", [128, BLK]) for b in range(NB)] for q in range(2)]
        SQ = [sb(f"SQ{b}", [128, BLK]) for b in range(NB)]
        ZB = [sb(f"ZB{b}", [P, TB, D + 1]) for b in range(NB)]
        ZQ = [sb(f"ZQ{b}", [P, TB, D]) for b in range(NB)]
        var3 = un[:, :, :].rearrange("p a h -> p (a h)")
        num3 = xl[:, :, :].rearrange("p a h -> p (a h)")
        gy = sb("gy", [P, COLS])
        slot2 = [sb(f"slotb{q}", [P, 2, TILES], i32) for q in range(2)]
        g2 = [sb(f"g2{q}", [P, 2, TILES, 2]) for q in range(2)]

        bank = [ctx.enter_context(nc.psum_tensor(f"bank{k}", [128, 512], f32)) for k in range(8)]
        psA = [[bank[2 * q + b] for b in range(NB)] for q in range(2)]
        psC, psV = bank[4], bank[5]
        psZ = [bank[6], bank[7]]
        acc = [bank[0], bank[1]]
        psT = [bank[2], bank[3]]
        psS = bank[4]

        s_ends, s_cate, s_cont, s_par, s_nch = sem("s_ends"), sem("s_cate"), sem("s_cont"), sem("s_par"), [sem("s_nch0"), sem("s_nch1")]
        s_tabT, s_v3 = sem("s_tabT"), sem("s_v3")
        s_iota, s_dve, s_rdy = sem("s_iota"), sem("s_dve"), sem("s_rdy")
        s_cmax, s_call, s_nr = sem("s_cmax"), sem("s_call"), sem("s_nr")
        s_nfree = sem("s_nfree")
        s_store = sem("s_store")
        s_cateh, s_cxn = sem("s_cateh"), sem("s_cxn")
        s_bs, s_bt, s_bsq, s_bv = sem("s_bs"), sem("s_bt"), sem("s_bsq"), sem("s_bv")
        s_wc, s_tps, s_tev = sem("s_wc"), sem("s_tps"), sem("s_tev")
        s_tmax, s_tall, s_misc, s_bqp, s_bqd = sem("s_tmax"), sem("s_tall"), sem("s_misc"), sem("s_bqp"), sem("s_bqd")
        s_tsc = sem("s_tsc")
        passes = ["deg"] + [f"l{l}" for l in range(LAYERS)]
        s_slot = {k: [sem(f"slot_ready_{k}{h}") for h in range(2)] for k in passes}
        s_gath = {k: [sem(f"gathered_{k}{h}") for h in range(2)] for k in passes[1:]}
        s_gused = {k: [sem(f"gath_used_{k}{h}") for h in range(2)] for k in passes[1:]}
        s_oh = {k: sem(f"onehots_ready_{k}") for k in passes}
        s_ohu = {k: sem(f"onehots_used_{k}") for k in passes}
        s_pass = sem("pass_done")
        s_accz = sem("acc_free")
        s_degm, s_degs = sem("deg_ready"), sem("deg_sqrt")
        s_utab, s_ust = sem("utab_ready"), sem("utab_stored")
        s_outt, s_outst = sem("out_ready"), sem("out_stored")
        t_cate = [sem(f"t_cate_loaded{q}") for q in range(2)]
        t_cx = [sem(f"t_cx_loaded{q}") for q in range(2)]
        t_oh, t_ohfree = sem("t_onehot_ready"), sem("t_onehot_free")
        t_A, t_Afree = sem("t_A_done"), sem("t_A_evacuated")
        t_C, t_Cfree = sem("t_C_done"), sem("t_C_evacuated")
        t_lo, t_x = sem("t_lo_copied"), sem("t_x_ready")
        t_sq, t_V, t_sd = sem("t_square_ready"), sem("t_V_done"), sem("t_sd_ready")
        t_xn, t_R = sem("t_xn_ready"), sem("t_R_ready")
        t_Z, t_zb, t_zq, t_red = sem("t_Z_done"), sem("t_zb_ready"), sem("t_zq_ready"), sem("t_zq_reduced")
        t_slot, t_g, t_gy = sem("t_slot_ready"), [sem("t_gathered0"), sem("t_gathered1")], sem("t_gy_added")
        s_fin, s_fs, s_y, s_out = sem("fin_var"), sem("fin_sqrt"), sem("fin_y"), sem("out_stored2")

        s_ext, s_zero = sem("extract"), sem("zeros_ready")
        s_gset, s_prep, s_sqs = sem("g_iotas"), sem("prep_done"), sem("bn_squares")
        t_rs = sem("t_rs_ready")
        s_own = {e: sem(f"carries_waits_{e}") for e in ("dve", "pool", "sp")}
        block = ctx.enter_context(nc.Block())

        def rows(v, n, parts):
            return v.rearrange("(o c) -> o c", o=1).broadcast_to([parts, n])

        NPAR = 16

        @block.sync
        def _(sp):
            sp.dma_start(ends[:, 0, :], src_e).then_inc(s_ends, 16)
            sp.dma_start(ends[:, 1, :], dst_e).then_inc(s_ends, 16)
            sp.dma_start(wf_s[:, :, :], rows(Wf, 3 * D, P).rearrange("p (a d) -> p a d", a=3)).then_inc(s_v3, 16)
            sp.dma_start(cont_f, cont.rearrange("s (c k) -> s c k", c=CONT)).then_inc(s_cont, 16)
            sp.dma_start(cate_i, cate).then_inc(s_cate, 16)
            n = 0

            def par(dst, src):
                sp.dma_start(dst, src).then_inc(s_par, 16)

            par(wc[:, :, :], Wc.rearrange("d (c k) -> d c k", c=CATE))
            par(bcb[:, :], rows(bc, D, P))
            par(bnp[:, 0, :], rows(bn_g, CONT, P))
            par(bnp[:, 1, :], rows(bn_b, CONT, P))
            par(wq[:, :], Wq)
            par(bqr[:, :], rows(bq, D, 1))
            for k, (g, b) in enumerate(((ln1_g, ln1_b), (ln2_g, ln2_b))):
                par(g12[D * k:D * k + D, :], g.rearrange("(c o) -> c o", o=1))
                par(b12[D * k:D * k + D, :], b.rearrange("(c o) -> c o", o=1))
            par(wm[:, 0:D], Wm)
            for k, v in enumerate((ln3_g, ln3_b, Wf[2 * D:3 * D], bm)):
                par(v3[:, k, :], rows(v, D, 128))
            par(bfb[:, :], rows(bf, 1, P))
            for c in range(NCH):
                if c == 2:
                    sp.wait_ge(s_cateh, 1)
                    sp.dma_start(cate16_d, cate_h).then_inc(s_store, 16)
                    sp.wait_ge(s_cxn, 1)
                    sp.dma_start(cxn_d.rearrange("s (c k) -> s c k", c=CONT), cont_f).then_inc(s_store, 16)
                    sp.wait_ge(s_store, 32)
                    sp.dma_start(tabT, tableT).then_inc(s_tabT, 16)
                if c >= 2:
                    sp.wait_ge(s_nfree, c - 1)
                sp.dma_start(nchunk[c % 2],
                             node_emb[:, c * CH * D:(c + 1) * CH * D].rearrange("p (c d) -> p c d", d=D)).then_inc(s_nch[c % 2], 16)
            for l in range(LAYERS):
                sp.wait_ge(s_utab, l + 1)
                sp.dma_start(u_d[l].rearrange("(p h) k -> p h k", p=P), utab).then_inc(s_ust, 16)
            sp.wait_ge(s_outt, 1)
            sp.dma_start(out_d.rearrange("(p h) k -> p h k", p=P), utab[:, :, 0:2]).then_inc(s_outst, 16)

            def load(i, q):
                sp.dma_start(cate_b[q],
                             cate16_d[ds(i, 1), :].broadcast_to([P, CATE * SB]).rearrange("p (c k) -> p c k", c=CATE)).then_inc(t_cate[q], 16)
                sp.dma_start(cx[q], cxn_d[ds(i, 1), :].rearrange("o (c k) -> (o c) k", c=CONT)).then_inc(t_cx[q], 16)

            def reload(i, q):
                sp.wait_ge(t_oh, (i - 1) * NKT)
                sp.sem_inc(s_own["sp"], 1)
                sp.wait_ge(t_C, (i - 1) * NB)
                sp.sem_inc(s_own["sp"], 1)
                load(i, q)

            sp.wait_ge(s_prep, 1)
            load(0, 0)
            load(1, 1)
            with sp.Fori(0, (NSB - 3) // 2) as it:
                reload(2 * it + 2, 0)
                reload(2 * it + 3, 1)
            reload(NSB - 1, (NSB - 1) % 2)
            sp.wait_ge(s_y, 1)
            sp.dma_start(y, gy[:, :]).then_inc(s_out, 16)
            sp.wait_ge(s_out, 16)

        @block.gpsimd
        def _(pool):
            nc.gpsimd.iota(iota_i[:, :, :], pattern=[[0, 2], [1, HALF]], base=0, channel_multiplier=0).then_inc(s_iota, 1)
            nc.gpsimd.iota(row_i[:, :], pattern=[[P, KT]], base=0, channel_multiplier=1).then_inc(s_iota, 1)
            pool.wait_ge(s_tmax, 1)
            nc.gpsimd.partition_all_reduce(tmax[:, 1:2], tmax[:, 0:1], 128, RMAX).then_inc(s_tall, 1)
            pool.wait_ge(s_cmax, 1)
            nc.gpsimd.partition_all_reduce(call[:, :], cmax[:, :], P, RMAX).then_inc(s_call, 1)
            pool.wait_ge(s_nr, 1)
            rounds = pool.value_load(nround[0:1, 0:1], min_val=1, max_val=ROUNDS_MAX)
            for l in range(LAYERS):
                k = f"l{l}"
                pool.wait_ge(s_ust, 16 * (l + 1))
                with pool.Fori(0, rounds) as r:
                    for h in range(2):
                        pool.wait_ge(s_slot[k][h], r + 1)
                        pool.sem_inc(s_own["pool"], 1)
                        for t in range(TOP):
                            nc.gpsimd.indirect_dma_start(
                                out=gath[h][:, t, :], out_offset=None, in_=u_d[l],
                                in_offset=bass.IndirectOffsetOnAxis(slot[h][:, 0, t:t + 1], 0)).then_inc(s_gath[k][h], 16)
            pool.wait_ge(s_outst, 16)

            def gathers(i, q):
                pool.wait_ge(t_slot, i + 1)
                pool.sem_inc(s_own["pool"], 1)
                for e in range(2):
                    for t in range(TILES):
                        nc.gpsimd.indirect_dma_start(
                            out=g2[q][:, e, t, :], out_offset=None, in_=out_d,
                            in_offset=bass.IndirectOffsetOnAxis(slot2[q][:, e, t:t + 1], 0)).then_inc(t_g[q], 16)

            gathers(0, 0)
            with pool.Fori(0, (NSB - 1) // 2) as it:
                gathers(2 * it + 1, 1)
                gathers(2 * it + 2, 0)

        @block.tensor
        def _(pe):
            mm = nc.tensor.matmul
            for k in range(2):
                pe.wait_ge(s_bs, k + 1)
                mm(psS[0:P, 8 * k:8 * k + CONT], lhsT=onesm[:, :], rhs=bstat[:, k, :], start=True, stop=True).then_inc(s_bt, 1)
            pe.wait_ge(s_bqp, 1)
            mm(psS[D:2 * D, 16:17], lhsT=bqr[:, :], rhs=one1[:, :], start=True, stop=True).then_inc(s_bqd, 1)
            pe.wait_ge(s_wc, 1)
            pe.wait_ge(s_tabT, 16)
            for j in range(KT):
                if j >= 2:
                    pe.wait_ge(s_tev, j - 1)
                mm(psT[j % 2][0:P, 0:CATE * D], lhsT=tabT[:, j * P:(j + 1) * P], rhs=wc[:, :, :].rearrange("d c k -> d (c k)"),
                   start=True, stop=True).then_inc(s_tps, 1)

            pe.wait_ge(s_zero, 1)
            pe.wait_ge(s_nr, 1)
            rounds = pe.value_load(nround[0:1, 0:1], min_val=1, max_val=ROUNDS_MAX)
            for n, k in enumerate(passes):
                if n:
                    pe.wait_ge(s_accz, n)
                for c in range(2):
                    mm(acc[c][0:P, 0:HI], lhsT=zero_l[:, :], rhs=iota16[:, :], start=True, stop=False,
                       skip_group_check=True).then_inc(s_ohu[k], 1)
                with pe.Fori(0, rounds) as r:
                    for t in range(ROUND):
                        pe.wait_ge(s_oh[k], r * ROUND + (t + 1))
                        for v in range(6 if n else 1):
                            last = mm(acc[v % 2][0:P, 0:HI], lhsT=oh_lo[t % 2][:, v, :], rhs=oh_hi[t % 2][:, :],
                                      start=False, stop=False, skip_group_check=True)
                        last.then_inc(s_ohu[k], 1)
                for c in range(2):
                    last = mm(acc[c][0:P, 0:HI], lhsT=zero_l[:, :], rhs=iota16[:, :], start=False, stop=True,
                              skip_group_check=True)
                last.then_inc(s_pass, 1)
            pe.wait_ge(s_accz, len(passes))
            pe.wait_ge(s_prep, 1)

            def feature_product(i, q, u, b):
                if b == 0:
                    pe.wait_ge(t_cx[q], 16 * (u + 1))
                pe.wait_ge(t_Cfree, i * NB + b)
                mm(psC[D:2 * D, 0:BLK], lhsT=wq[:, :], rhs=cx[q][:, b * BLK:(b + 1) * BLK],
                   start=True, stop=True).then_inc(t_C, 1)

            def variances(i, b):
                pe.wait_ge(t_sq, i * NB + b + 1)
                pe.wait_ge(t_sd, i * NB + b)
                mm(psV[:, 0:BLK], lhsT=blockones[:, :], rhs=SQ[b][:, :], start=True, stop=True).then_inc(t_V, 1)

            def last_product(i, b):
                pe.wait_ge(t_R, i * NB + b + 1)
                pe.wait_ge(t_zb, i * NB)
                for t in range(TB):
                    last = mm(psZ[b][0:P, t * (D + 1):(t + 1) * (D + 1)], lhsT=R[b][:, t * P:(t + 1) * P], rhs=wm[:, :],
                              start=True, stop=True, skip_group_check=True)
                last.then_inc(t_Z, 1)

            def superblock(i, q, u, prev):
                for kt in range(NKT):
                    c, j = kt // KT, kt % KT
                    pe.wait_ge(t_oh, i * NKT + (kt + 1))
                    for b in range(NB):
                        if kt == 0:
                            pe.wait_ge(t_Afree, i * NB + b + 1)
                        last = mm(psA[q][b][:, 0:BLK], lhsT=T16[:, j, c, :], rhs=onehot[kt % RING][:, b * BLK:(b + 1) * BLK],
                                  start=kt == 0, stop=kt == NKT - 1)
                        if kt == NKT - 1 and b == 0:
                            last.then_inc(t_A, 1)
                    last.then_inc(t_ohfree, 1)
                    if prev and kt in (8, 12):
                        variances(i - 1, kt == 12)
                    if kt in (16, 40):
                        feature_product(i, q, u, int(kt == 40))
                    if prev and kt in (26, 30):
                        last_product(i - 1, kt == 30)

            superblock(0, 0, 0, False)
            with pe.Fori(0, (NSB - 1) // 2) as it:
                superblock(2 * it + 1, 1, it, True)
                superblock(2 * it + 2, 0, it + 1, True)
            for b in range(NB):
                variances(NSB - 1, b)
            for b in range(NB):
                last_product(NSB - 1, b)

        @block.scalar
        def _(act):
            A = nc.scalar.activation
            for c in range(CONT):
                act.wait_ge(s_bsq, c + 1)
                if c:
                    act.wait_ge(s_sqs, c)
                A(sqj[:, :], cont_f[:, c, :], ACT.Square, accum_out=bstat[:, 1, c:c + 1]).then_inc(s_sqs, 1)
            act.wait_ge(s_bv, 1)
            A(bstat[:, 3, :], bstat[:, 2, :], ACT.Sqrt).then_inc(s_bv, 1)
            act.wait_ge(s_degm, 1)
            A(degm[:, :], degm[:, :], ACT.Sqrt).then_inc(s_degs, 1)
            act.wait_ge(s_prep, 1)

            def feature_evac(i, q, b):
                act.wait_ge(t_C, i * NB + b + 1)
                if not isinstance(i, int):
                    act.wait_ge(t_xn, (i - 1) * NB)
                A(X[q][b][D:2 * D, :], psC[D:2 * D, 0:BLK], ACT.Identity, bias=bqc[D:2 * D, :]).then_inc(t_Cfree, 1)

            def lo_copies(i, q):
                for b in range(NB):
                    if b == 0:
                        act.wait_ge(t_A, i + 1)
                    else:
                        act.wait_ge(t_ohfree, (i + 1) * NKT + RING)
                    act.wait_ge(t_x, i * NB)
                    A(lo_part[b], psA[q][b][D:2 * D, 0:BLK], ACT.Copy, scale=sc_i[0:D, 0:1].bitcast(f32)).then_inc(t_lo, 1)

            def squares(i, q):
                for b in range(NB):
                    act.wait_ge(t_x, i * NB + b + 1)
                    act.wait_ge(t_Cfree, i * NB + b + 1)
                    act.wait_ge(t_V, i * NB)
                    A(SQ[b][:, :], X[q][b][:, :], ACT.Square).then_inc(t_sq, 1)

            def deviations(i):
                for b in range(NB):
                    act.wait_ge(t_V, i * NB + b + 1)
                    act.wait_ge(t_xn, i * NB)
                    A(SD[b], psV[:, 0:BLK], ACT.Sqrt, bias=eps[:, :]).then_inc(t_sd, 1)

            def relus(i):
                for b in range(NB):
                    act.wait_ge(t_xn, i * NB + b + 1)
                    act.wait_ge(t_Z, i * NB)
                    A(R[b], SD[b], ACT.Relu, scale=g12[:, :], bias=b12[:, :]).then_inc(t_R, 1)

            def last_squares(i):
                for b in range(NB):
                    act.wait_ge(t_zb, i * NB + b + 1)
                    act.wait_ge(t_red, i * NB)
                    A(ZQ[b][:, :, :], ZB[b][:, :, 0:D], ACT.Square).then_inc(t_zq, 1)

            def superblock(i, q):
                lo_copies(i - 1, 1 - q)
                squares(i - 1, 1 - q)
                deviations(i - 1)
                feature_evac(i, q, 0)
                relus(i - 1)
                feature_evac(i, q, 1)
                last_squares(i - 1)

            feature_evac(0, 0, 0)
            feature_evac(0, 0, 1)
            with act.Fori(0, (NSB - 1) // 2) as it:
                superblock(2 * it + 1, 1)
                superblock(2 * it + 2, 0)
            q = (NSB - 1) % 2
            lo_copies(NSB - 1, q)
            squares(NSB - 1, q)
            deviations(NSB - 1)
            relus(NSB - 1)
            last_squares(NSB - 1)
            act.wait_ge(s_fin, 1)
            A(var3, var3, ACT.Sqrt, scale=1.0 / D, bias=eps[0:P, :]).then_inc(s_fs, 1)

        @block.vector
        def _(dve):
            V = nc.vector
            chain = [0]

            def link(ins):
                chain[0] += 1
                ins.then_inc(s_dve, 1)
                dve.wait_ge(s_dve, chain[0])

            V.memset(onesm[:, :], 1.0)
            dve.wait_ge(s_cont, 16)
            V.tensor_reduce(bstat[:, 0, :], cont_f, AX.X, ALU.add).then_inc(s_bs, 1)
            dve.wait_ge(s_cate, 16)
            V.tensor_copy(cate_h, cate_i).then_inc(s_cateh, 1)
            dve.wait_ge(s_bt, 1)
            link(V.tensor_scalar(bstat[:, 0, :], psS[0:P, 0:CONT], 1.0 / E, None, ALU.mult))
            for c in range(CONT):
                V.tensor_scalar(cont_f[:, c, :], cont_f[:, c, :], bstat[:, 0, c:c + 1], None, ALU.subtract).then_inc(s_bsq, 1)
            dve.wait_ge(s_sqs, CONT)
            link(V.tensor_copy(bstat[:, 1, :], bstat[:, 1, :]))
            dve.sem_inc(s_bs, 1)
            dve.wait_ge(s_bt, 2)
            V.tensor_scalar(bstat[:, 2, :], psS[0:P, 8:8 + CONT], 1.0 / E, EPS, ALU.mult, ALU.add).then_inc(s_bv, 1)
            dve.wait_ge(s_bv, 2)
            link(V.reciprocal(bstat[:, 3, :], bstat[:, 3, :]))
            dve.wait_ge(s_par, 16 * NPAR)
            link(V.tensor_tensor(bnp[:, 0, :], bnp[:, 0, :], bstat[:, 3, :], ALU.mult))
            for c in range(CONT):
                last = V.tensor_scalar(cont_f[:, c, :], cont_f[:, c, :], bnp[:, 0, c:c + 1], bnp[:, 1, c:c + 1], ALU.mult, ALU.add)
            last.then_inc(s_cxn, 1)

            def centre(w, parts, n, out=None):
                s = wsum[0:parts, 0:1]
                link(V.tensor_reduce(s, w, AX.X, ALU.add))
                link(V.tensor_scalar(s, s, 1.0 / n, None, ALU.mult))
                link(V.tensor_scalar(w, w, s, None, ALU.subtract))

            for c in range(CATE):
                centre(wc[:, c, :], D, D)
            dve.sem_inc(s_wc, 1)
            centre(wq[:, :], CONT, D)
            centre(bcb[:, :], P, D)
            V.memset(one1[:, :], 1.0)
            centre(bqr[:, :], 1, D)
            dve.sem_inc(s_bqp, 1)
            centre(wm[:, 0:D], 128, D)
            V.memset(eps[:, :], EPS)
            link(V.memset(blockones[:, :], 0.0))
            for k in range(2):
                V.memset(blockones[k * D:(k + 1) * D, k * D:(k + 1) * D], 1.0 / D)
            link(V.tensor_tensor(gw[:, :], v3[:, 0, :], v3[:, 2, :], ALU.mult))
            link(V.tensor_tensor(wtmp[:, :], wm[:, 0:D], gw[:, :], ALU.mult))
            link(V.tensor_reduce(wm[:, D:D + 1], wtmp[:, :], AX.X, ALU.add))
            link(V.tensor_copy(brow[:, 0:D], v3[0:P, 3, :]))
            centre(brow[:, 0:D], P, D)
            link(V.tensor_tensor(wtmp[0:P, :], brow[:, 0:D], gw[0:P, :], ALU.mult))
            link(V.tensor_reduce(brow[:, D:D + 1], wtmp[0:P, :], AX.X, ALU.add))
            link(V.tensor_tensor(wtmp[0:P, :], v3[0:P, 1, :], v3[0:P, 2, :], ALU.mult))
            link(V.tensor_reduce(k0[:, 0:1], wtmp[0:P, :], AX.X, ALU.add))
            link(V.tensor_tensor(k0[:, 1:2], k0[:, 0:1], bfb[:, :], ALU.add))
            dve.wait_ge(s_bqd, 1)
            V.tensor_copy(bqc[D:2 * D, :], psS[D:2 * D, 16:17])

            link(V.memset(tmax[:, :], 0.0))
            for j in range(KT):
                dve.wait_ge(s_tps, j + 1)
                ins = V.tensor_copy(Tf[:, j, :, :], psT[j % 2][0:P, 0:CATE * D].rearrange("p (c d) -> p c d", c=CATE))
                ins.then_inc(s_tev, 1)
            dve.wait_ge(s_tev, KT)
            link(V.memset(Tf[0:1, 0, :, :], 0.0))
            link(V.tensor_tensor(Tf[:, :, 0, :], Tf[:, :, 0, :],
                                 bcb[:, :].rearrange("p (o d) -> p o d", o=1).broadcast_to([P, KT, D]), ALU.add))
            V.tensor_reduce(tmax[0:P, 0:1], Tf, AX.XYZ, ALU.max, apply_absolute_value=True).then_inc(s_tmax, 1)
            dve.wait_ge(s_tall, 1)
            link(V.tensor_scalar(sc_i[:, 0:1], tmax[:, 1:2].bitcast(i32), 0x7F800000, None, ALU.bitwise_and))
            link(V.tensor_scalar(sc_i[:, 0:1], sc_i[:, 0:1], -13.0 * 2 ** 23, float(2 ** 23), ALU.add, ALU.max))
            link(V.tensor_scalar(sc_i[:, 1:2], sc_i[:, 0:1], -1.0, 254.0 * 2 ** 23, ALU.mult, ALU.add))
            Tv = Tf.rearrange("p j c d -> p (j c) d")
            T16v = T16[:, :, :, :].rearrange("p j c d -> p (j c) d")
            link(V.tensor_scalar(Tv, Tv, sc_i[0:P, 1:2].bitcast(f32), None, ALU.mult))
            link(V.tensor_copy(T16v[:, :, 0:D], Tv))
            link(V.tensor_tensor(T16v[:, :, D:2 * D], Tv, T16v[:, :, 0:D], ALU.subtract))
            dve.wait_ge(s_store, 32)
            dve.sem_inc(s_prep, 1)

            dve.wait_ge(s_v3, 16)
            for ch in range(NCH):
                dve.wait_ge(s_nch[ch % 2], 16 * (ch // 2 + 1))
                for k in range(2):
                    ins = V.tensor_tensor(nprod[k], nchunk[ch % 2],
                                          wf_s[:, k:k + 1, :].broadcast_to([P, CH, D]), ALU.mult)
                    if k == 1:
                        ins.then_inc(s_nfree, 1)
                    else:
                        link(ins)
                dve.wait_ge(s_nfree, ch + 1)
                for k in range(2):
                    ins = V.tensor_reduce(xnode[:, k, ch * CH:(ch + 1) * CH], nprod[k], AX.X, ALU.add)
                link(ins)

            dve.wait_ge(s_iota, 2)
            V.tensor_copy(row_f[:, :], row_i[:, :])
            V.tensor_copy(iota16[:, :], iota_i[:, 0, :])
            V.memset(zero_l[:, :], 0.0).then_inc(s_zero, 1)
            link(V.tensor_scalar(col_key, iota_i[:, :, :], -256.0, 65536.0, ALU.add, ALU.mult))
            dve.wait_ge(s_ends, 32)
            link(V.tensor_copy(dst_f, ends[:, 1, :]))
            link(V.tensor_scalar(valid, dst_f, float(N), None, ALU.is_lt))
            V.tensor_scalar(ends[:, 1, :], dst_f, float(N - 1), None, ALU.min)
            link(V.tensor_reduce(cnt[:, :], valid.rearrange("p (h c) -> p h c", h=2), AX.X, ALU.add))
            V.tensor_reduce(cmax[:, :], cnt[:, :], AX.X, ALU.max).then_inc(s_cmax, 1)
            flat = "p h c -> p (h c)"
            link(V.memset(keys[:, 0, :, :], FILL_SRC))
            link(V.memset(keys[:, 1, :, :], FILL_DST))
            link(V.tensor_tensor(dst_f, dst_f, col_key.rearrange(flat), ALU.add))
            link(V.copy_predicated(keys[:, 1, :, :].rearrange(flat), valid, dst_f))
            link(V.tensor_tensor(dst_f, ends[:, 0, :], col_key.rearrange(flat), ALU.add))
            link(V.copy_predicated(keys[:, 0, :, :].rearrange(flat), valid, dst_f))
            link(V.memset(packed[:, 0, :], FILL_SRC))
            link(V.memset(packed[:, 1, :], FILL_DST))
            dve.wait_ge(s_call, 1)
            link(V.tensor_scalar(nround[:, 1:2], call[:, :], float(TOP - 1), float(TOP), ALU.add, ALU.max))
            V.tensor_scalar(nround[:, 0:1], nround[:, 1:2], 3, None, ALU.arith_shift_right).then_inc(s_nr, 1)
            dve.wait_ge(s_nr, 1)
            rounds = dve.value_load(nround[0:1, 0:1], min_val=1, max_val=ROUNDS_MAX)

            with dve.Fori(0, rounds) as r:
                dve.wait_ge(s_ext, r * 9)
                dve.sem_inc(s_own["dve"], 1)
                for a in range(2):
                    for h in range(2):
                        V.max(top8[:, a, h, :], keys[:, a, h, :]).then_inc(s_ext, 1)
                dve.wait_ge(s_ext, r * 9 + 4)
                V.tensor_copy(packed[:, :, ds(r * ROUND, ROUND)], top8[:, :, :, :].rearrange("p a h t -> p a (h t)")).then_inc(s_ext, 1)
                for a in range(2):
                    for h in range(2):
                        V.match_replace(keys[:, a, h, :], top8[:, a, h, :], keys[:, a, h, :], (FILL_SRC, FILL_DST)[a]).then_inc(s_ext, 1)
            dve.wait_ge(s_ext, rounds * 9)
            link(V.tensor_copy(packed_i, packed[:, :, :]))
            link(V.tensor_scalar(packed_i, packed_i, 0xFFFF, None, ALU.bitwise_and))
            V.tensor_copy(tri[:, 0, :], packed_i[:, 0, :])
            pdst, plo, phi = packed[:, 0, :], tri[:, 1, :].bitcast(f32), tri[:, 2, :].bitcast(f32)
            MAGIC = 1.5 * 2 ** 23
            link(V.tensor_copy(pdst, packed_i[:, 1, :]))
            link(V.tensor_scalar(plo, pdst, -(HI - 1) / 2, 1.0 / HI, ALU.add, ALU.mult))
            link(V.tensor_scalar(plo, plo, MAGIC, None, ALU.add))
            link(V.tensor_scalar(plo, plo, MAGIC, None, ALU.subtract))
            link(V.scalar_tensor_tensor(phi, plo, -float(HI), pdst, ALU.mult, ALU.add))

            io_lo, io_hi = iota16[:, 0:P], iota16[:, :]
            for n, k in enumerate(passes):
                def fill_slot(h, r):
                    V.tensor_copy(slot[h][:, :, :], tri[:, :, ds(r * ROUND + h * TOP, TOP)]).then_inc(s_slot[k][h], 1)

                fill_slot(0, 0)
                with dve.Fori(0, rounds) as r:
                    for h in range(2):
                        dve.wait_ge(s_slot[k][h], r + 1)
                        if n:
                            dve.wait_ge(s_gath[k][h], (r + 1) * 16 * TOP)
                        lo = slot[h][:, 1, :].bitcast(f32)
                        hi = slot[h][:, 2, :].bitcast(f32)
                        for t in range(TOP):
                            dve.wait_ge(s_ohu[k], r * ROUND + (h * TOP + t + 1))
                            V.tensor_scalar(oh_hi[t % 2][:, :], io_hi, hi[:, t:t + 1], None, ALU.is_equal)
                            if n == 0:
                                last = V.tensor_scalar(oh_lo[t % 2][:, 0, :], io_lo, lo[:, t:t + 1], None, ALU.is_equal)
                            else:
                                for v in range(6):
                                    last = V.tensor_scalar(oh_lo[t % 2][:, v, :], io_lo, lo[:, t:t + 1], gath[h][:, t, v:v + 1],
                                                           ALU.is_equal, ALU.mult)
                            last.then_inc(s_oh[k], 1)
                            if t == 0:
                                dve.wait_ge(s_oh[k], r * ROUND + h * TOP)
                                fill_slot(1 - h, r + h)
                dve.wait_ge(s_pass, n + 1)
                disb = dis[:, :].rearrange("p (o h) -> p o h", o=1).broadcast_to([P, 2, HI])
                if n == 0:
                    V.tensor_scalar(degm[:, :], acc[0][0:P, 0:HI], 1.0, None, ALU.max).then_inc(s_degm, 1)
                    V.tensor_scalar(dis[:, :], acc[0][0:P, 0:HI], 0.0, None, ALU.is_gt).then_inc(s_accz, 1)
                    dve.wait_ge(s_accz, 1)
                    dve.wait_ge(s_degs, 1)
                    link(V.reciprocal(degm[:, :], degm[:, :]))
                    link(V.tensor_tensor(dis[:, :], dis[:, :], degm[:, :], ALU.mult))
                    V.tensor_scalar(outn[:, :, :], xnode[:, :, :], 1.0 / (LAYERS + 1), None, ALU.mult)
                    src = xnode
                else:
                    for c in range(2):
                        ins = V.tensor_tensor(xl[:, c, :], acc[c][0:P, 0:HI], dis[:, :], ALU.mult)
                        if c:
                            ins.then_inc(s_accz, 1)
                    dve.wait_ge(s_accz, n + 1)
                    link(V.scalar_tensor_tensor(outn[:, :, :], xl[:, :, :], 1.0 / (LAYERS + 1), outn[:, :, :], ALU.mult, ALU.add))
                    src = xl
                if n < LAYERS:
                    if n:
                        dve.wait_ge(s_ust, 16 * n)
                    link(V.tensor_tensor(un[:, :, :], src[:, :, :], disb, ALU.mult))
                    for part in range(3):
                        dst = utab[:, :, 2 * part:2 * part + 2].rearrange("p h a -> p a h")
                        link(V.tensor_copy(part_b[:, :, :], un[:, :, :]))
                        link(V.tensor_copy(dst, part_b[:, :, :]))
                        if part < 2:
                            link(V.tensor_tensor(un[:, :, :], un[:, :, :], part_b[:, :, :], ALU.subtract))
                    dve.sem_inc(s_utab, 1)
                else:
                    dve.wait_ge(s_ust, 16 * LAYERS)
                    V.tensor_copy(utab[:, :, 0:2].rearrange("p h a -> p a h"), outn[:, :, :]).then_inc(s_outt, 1)

            def index_slot(i, q):
                V.tensor_copy(slot2[q][:, :, :], ends[:, :, ds(i * TILES, TILES)]).then_inc(t_slot, 1)

            def add_gathered(i, q, u):
                dve.wait_ge(t_g[q], 16 * 2 * TILES * (u + 1))
                V.tensor_tensor(gy[:, ds(i * TILES, TILES)], g2[q][:, 0, :, 0], g2[q][:, 1, :, 1], ALU.add).then_inc(t_gy, 1)

            def add_parts(i, q, b):
                dve.wait_ge(t_lo, i * NB + b + 1)
                V.scalar_tensor_tensor(X[q][b][0:D, :], psA[q][b][0:D, 0:BLK], sc_i[0:D, 0:1].bitcast(f32),
                                       lo_part[b], ALU.mult, ALU.add).then_inc(t_x, 1)
                dve.wait_ge(t_x, i * NB + b + 1)
                dve.sem_inc(t_Afree, 1)

            def normalise(i, q, b):
                dve.wait_ge(t_sd, i * NB + b + 1)
                V.reciprocal(SD[b], SD[b]).then_inc(t_rs, 1)
                dve.wait_ge(t_rs, i * NB + b + 1)
                V.tensor_tensor(SD[b], X[q][b][:, :], SD[b], ALU.mult).then_inc(t_xn, 1)

            def last_bias(i, b):
                dve.wait_ge(t_Z, i * NB + b + 1)
                dve.wait_ge(t_zq, i * NB)
                V.tensor_tensor(ZB[b][:, :, :], psZ[b][0:P, 0:TB * (D + 1)].rearrange("p (t d) -> p t d", t=TB),
                                brow[:, :].rearrange("p (o d) -> p o d", o=1).broadcast_to([P, TB, D + 1]), ALU.add).then_inc(t_zb, 1)
                dve.wait_ge(t_zb, i * NB + b + 1)
                V.tensor_copy(num3[:, ds(i * TILES + b * TB, TB)], ZB[b][:, :, D])

            def last_variance(i, b):
                dve.wait_ge(t_zq, i * NB + b + 1)
                V.tensor_reduce(var3[:, ds(i * TILES + b * TB, TB)], ZQ[b][:, :, :], AX.X, ALU.add).then_inc(t_red, 1)

            dve.sem_inc(t_ohfree, RING)
            dve.sem_inc(t_Afree, 2 * NB)

            def superblock(i, q, u, prev, up):
                dve.wait_ge(t_cate[q], 16 * (u + 1))
                for kt in range(NKT):
                    c, j = kt // KT, kt % KT
                    dve.wait_ge(t_ohfree, i * (NKT) + (kt + 1))
                    V.tensor_scalar(onehot[kt % RING], cate_b[q][:, c, :], row_f[:, j:j + 1], None, ALU.is_equal).then_inc(t_oh, 1)
                    if kt == 5:
                        index_slot(i, q)
                    if prev:
                        if kt in (1, 3):
                            add_parts(i - 1, 1 - q, kt == 3)
                        if kt in (20, 24):
                            normalise(i - 1, 1 - q, kt == 24)
                        if kt in (38, 42):
                            last_bias(i - 1, kt == 42)
                        if kt in (46, 48):
                            last_variance(i - 1, kt == 48)
                        if kt == 4:
                            add_gathered(i - 1, 1 - q, up)

            superblock(0, 0, 0, False, 0)
            with dve.Fori(0, (NSB - 1) // 2) as it:
                superblock(2 * it + 1, 1, it, True, it)
                superblock(2 * it + 2, 0, it + 1, True, it)
            i, q = NSB - 1, (NSB - 1) % 2
            add_gathered(i, q, i // 2)
            for step in (lambda b: add_parts(i, q, b), lambda b: normalise(i, q, b), lambda b: last_bias(i, b),
                         lambda b: last_variance(i, b)):
                for b in range(NB):
                    step(b)
            dve.wait_ge(t_red, NSB * NB)
            dve.sem_inc(s_fin, 1)
            dve.wait_ge(t_gy, NSB)
            link(V.tensor_scalar(gy[:, :], gy[:, :], k0[:, 1:2], None, ALU.add))
            dve.wait_ge(s_fs, 1)
            link(V.reciprocal(var3, var3))
            link(V.tensor_tensor(num3, num3, var3, ALU.mult))
            V.tensor_tensor(gy[:, :], gy[:, :], num3, ALU.add).then_inc(s_y, 1)


def kernel(**inputs):
    import numpy as _np
    import concourse.bacc as _bacc
    from concourse import mybir as _mybir
    from concourse.bass_utils import run_bass_kernel_spmd as _run

    a = {k.replace("L0_rec_", ""): _np.ascontiguousarray(v) for k, v in inputs.items()}
    edges = a["r_edge_index"]
    by_superblock = lambda x: _np.ascontiguousarray(
        x.reshape(x.shape[0], P, NSB, TILES).transpose(2, 0, 3, 1).reshape(NSB, -1))
    arrays = {
        "src": edges[0].reshape(P, COLS), "dst": edges[1].reshape(P, COLS),
        "cate": by_superblock(a["r_cate_features"]), "cont": by_superblock(a["cont_features"]),
        "node": a["node_emb"].reshape(P, HI * D), "tabT": _np.ascontiguousarray(a["cate_table"].T),
        "Wc": _np.ascontiguousarray(a["Wc"].reshape(CATE, D, D).transpose(1, 0, 2).reshape(D, CATE * D)),
        "bc": a["bc"], "ln1_g": a["ln1_g"], "ln1_b": a["ln1_b"], "bn_g": a["bn_g"], "bn_b": a["bn_b"],
        "Wq": a["Wq"], "bq": a["bq"], "ln2_g": a["ln2_g"], "ln2_b": a["ln2_b"], "Wm": a["Wm"], "bm": a["bm"],
        "ln3_g": a["ln3_g"], "ln3_b": a["ln3_b"], "Wf": a["Wf"].reshape(3 * D), "bf": a["bf"],
    }
    nc = _bacc.Bacc("TRN2", target_bir_lowering=False, num_devices=1)
    args = []
    for name, x in arrays.items():
        args.append(nc.dram_tensor(f"in_{name}", x.shape, _mybir.dt.from_np(x.dtype), kind="ExternalInput").ap())
    args.append(nc.dram_tensor("out_y", (P, COLS), _mybir.dt.float32, kind="ExternalOutput").ap())
    rec_kernel(nc, *args)
    r = _run(nc, [{f"in_{k}": v for k, v in arrays.items()}], core_ids=[0])
    return r.results[0]["out_y"].reshape(E)
```

```python
import concourse.bass as bass
from concourse import mybir
from contextlib import ExitStack
import numpy as np

N = 62500
D = 64
E = 125000
OFF = 1250
CATE = 5
CONT = 8
LAYERS = 3
EPS = 1e-5
P = 125
COLS = E // P
HI = N // P
HALF = COLS // 2
TOP = 8
ROUND = 2 * TOP
ROUNDS_MAX = -(-HALF // TOP)
RS = 12
LISTW = (ROUNDS_MAX + 1) * ROUND
FILL_SRC = -float(2 ** 25)
FILL_DST = -float(2 ** 25) + 65534.0
SB = 1000
TILES = SB // P
NSB = E // SB
BLK = 500
NB = SB // BLK
KT = OFF // P
NKT = CATE * KT
RING = 10
GR = 4
TB = BLK // P
PRIME = 1
LOADED = (2, 3, 4)
CATS = (4, 3, 2)
GATHERED = dict(deg=((0, 1, 2), (0, 1, 2)), layer=((0, 1), (0,)), nodes=((0, 1), (0, 1)), tail=((0, 1), (0, 1)))
TAIL_PAIRS = 5
GSTEP = 10
XROWS = 6 * CONT
XPARTS = ((0, 0), (0, 1), (0, 2), (1, 0), (1, 1), (2, 0))
AT_PE = dict(variance=(8, 13), feature=(19, 26), product=(21, 28))
AT_ACT = dict(lo=(0, 1), square=(3, 4), rstd=(9, 14), relu=(12, 17), feature=(20, 27), zsquare=(24, 31))
AT_DVE = dict(parts=(10, 12), normalise=(21, 26), bias=(32, 39), zvariance=(41, 46))
AT_CATS = (24, 40, 46)
AT_TILE = [5 + 44 * t // (ROUND - 1) for t in range(ROUND)]
ACT_LEAD = 8
BN_CHUNKS = (6, 11)
F_MAX = 13


def rec_kernel(nc, src_e, dst_e, cate, cate_tiles, cont, node_emb, tableT, Wc, bc, ln1_g, ln1_b, bn_g, bn_b,
               Wq6, partmask, bq, ln2_g, ln2_b, Wm, bm, ln3_g, ln3_b, Wf, bf, y):
    f32, bf16, f16, i32 = mybir.dt.float32, mybir.dt.bfloat16, mybir.dt.float16, mybir.dt.int32
    ALU, ACT, AX = mybir.AluOpType, mybir.ActivationFunctionType, mybir.AxisListType
    RMAX = bass.bass_isa.ReduceOp.max
    ds = bass.ds
    ctx = ExitStack()
    with ctx:
        def sb(name, shape, dt=f32):
            return ctx.enter_context(nc.sbuf_tensor(name, shape, dt))

        def sem(name):
            return ctx.enter_context(nc.semaphore(name))

        cate16_d = nc.dram_tensor("cate16_d", [NSB, CATE * SB], f16, kind="Internal").ap()
        T16_d = [nc.dram_tensor(f"T16_{c}_d", [OFF, 2 * D], f16, kind="Internal").ap() for c in CATS]
        cxp_d = [nc.dram_tensor(f"cxp{k}_d", [NSB, CONT * SB], bf16, kind="Internal").ap() for k in range(3)]
        u_d = [nc.dram_tensor(f"u{l}_d", [N, 4], f32, kind="Internal").ap() for l in range(LAYERS)]
        out_d = nc.dram_tensor("out_d", [N, 2], f32, kind="Internal").ap()
        yd_d = nc.dram_tensor("yd_d", [E, 1], f32, kind="Internal").ap()

        def views(area):
            at = [0]

            def take(shape, dt=f32):
                words = int(np.prod(shape[1:])) * (2 if dt in (f16, bf16) else 4) // 4
                v = area[0:shape[0], at[0]:at[0] + words]
                at[0] += words
                assert at[0] <= area.shape[1], (at[0], area.shape)
                if dt != f32:
                    v = v.bitcast(dt)
                if len(shape) > 2:
                    names = "abcd"[:len(shape) - 1]
                    v = v.rearrange(f"p ({' '.join(names)}) -> p {' '.join(names)}", **dict(zip(names, shape[1:])))
                return v
            return take

        wide = sb("wide", [128, 15500])
        take = views(wide)
        cont_f = take([P, CONT, SB])
        cate_i = take([P, CATE * SB], i32)
        cate_h = take([P, CATE * SB], f16)
        take = views(wide)
        take([P, CONT * SB])
        cont_part = take([P, CONT, SB], bf16)
        take = views(wide)
        onehot = [take([P, SB], f16) for _ in range(RING)]
        cate_b = [take([P, CATE, SB], f16) for _ in range(2)]
        lo_part = [take([D, BLK]) for _ in range(NB)]
        SD = [take([128, BLK]) for _ in range(NB)]
        R = [take([128, BLK]) for _ in range(NB)]
        cx = [take([XROWS, SB], bf16) for _ in range(2)]
        rowsT = [take([P, TILES, 2 * D], f16) for _ in CATS[:2]]
        listmem = sb("listmem", [P, 5 * LISTW])
        take = views(listmem)
        tabT = take([D, OFF])
        Tf = take([P, KT, CATE, D])
        take = views(listmem)
        col_key = take([P, 2, HALF])
        valid = take([P, COLS], i32)
        dst_f = take([P, COLS])
        packed = views(listmem)([P, 5, LISTW], i32)
        CH = 20
        NCH = HI // CH
        nodemem = sb("nodemem", [P, 2 * CH * D])
        take = views(nodemem)
        nchunk = [take([P, CH, D]) for _ in range(2)]
        take = views(nodemem)
        utab = take([P, HI, 4])
        rowsT.append(take([P, TILES, 2 * D], f16))
        otab = views(nodemem)([P, HI, 2])

        ends = sb("ends", [P, 2, COLS], i32)
        keys = sb("keys", [P, 2, 2, HALF])
        top8 = sb("top8", [P, 2, 2, TOP])
        pk = sb("pk", [P, 2, ROUND])
        pk_i = sb("pk_i", [P, 2, ROUND], i32)
        pk_c = sb("pk_c", [P, ROUND], i32)
        pk_f = sb("pk_f", [P, 2, ROUND])
        rnd = sb("rnd", [P, 5, ROUND], i32)
        ebase = sb("ebase", [P, ROUND])
        ebase_i = sb("ebase_i", [P, ROUND], i32)
        cnt = sb("cnt", [P, 2])
        cmax = sb("cmax", [P, 1])
        call = sb("call", [P, 1])
        nround = sb("nround", [P, 3], i32)
        slot = [sb(f"slot{h}", [P, TOP], i32) for h in range(2)]
        slotd = [sb(f"slotd{h}", [P, 2, TOP], i32) for h in range(2)]
        gath = [sb(f"gath{h}", [P, TOP, 4]) for h in range(2)]
        oh_hi = [sb(f"oh_hi{k}", [P, HI], f16) for k in range(GR)]
        oh_lo8 = [sb(f"oh_lo8{h}", [P, TOP, P], f16) for h in range(2)]
        oh_lo = [sb(f"oh_lo{k}", [P, 4, P], f16) for k in range(GR)]
        iota_i = sb("iota_i", [P, 2, HALF], i32)
        iota16 = sb("iota16", [P, HI], f16)
        zero_l = sb("zero_l", [P, P], f16)
        slot_c = [sb(f"slot_cate{q}", [P, len(CATS), TILES], i32) for q in range(2)]
        ident16 = sb("ident16", [P, P], f16)
        ident = sb("ident", [P, P])
        w4 = sb("w4", [128, 4])
        xT = [sb(f"xT{k}", [128, 4 * P]) for k in range(2)]
        xnode = sb("xnode", [P, 2, HI])
        outn = sb("outn", [P, 2, HI])
        dis = sb("dis", [P, HI])
        degm = sb("degm", [P, HI])
        un = sb("un", [P, 2, HI])
        xl = sb("xl", [P, 2, HI])
        part_h = sb("part_h", [P, 2, HI], f16)
        umax = sb("umax", [P, 2])
        us_i = sb("us_i", [P, 2], i32)
        slot_d2 = [sb(f"slot_dst{h}", [P, 2, TOP], i32) for h in range(2)]
        gd = [sb(f"gd{h}", [P, TOP, 2]) for h in range(2)]
        slot_s = [sb(f"slot_src{q}", [P, GSTEP], i32) for q in range(2)]
        gs = [sb(f"gs{q}", [P, GSTEP, 2]) for q in range(2)]
        dlast = sb("dlast", [P, 1])
        ys = sb("ys", [P, COLS])
        yd = sb("yd", [P, COLS])

        bstat = sb("bstat", [P, 4, CONT])
        sqj = sb("sqj", [P, SB])
        bnp = sb("bnp", [P, 2, CONT])
        onesm = sb("onesm", [P, P])
        pidx_i = sb("pidx_i", [P, 1], i32)
        pidx = sb("pidx", [P, 1])
        wc = sb("wc", [D, CATE, D])
        wsum = sb("wsum", [128, 8])
        T16 = sb("T16", [P, KT, CATE, 2 * D], f16)
        bcb = sb("bcb", [P, D])
        tmax = sb("tmax", [128, 2])
        sc_i = sb("sc_i", [128, 2], i32)
        wq6 = sb("wq6", [XROWS, D])
        wqp = sb("wqp", [XROWS, 3, D], bf16)
        wqx = sb("wqx", [XROWS, D], bf16)
        wqr = sb("wqr", [XROWS, D])
        pmask = sb("pmask", [XROWS, 3])
        bqr = sb("bqr", [1, D])
        one1 = sb("one1", [1, 1])
        bqc = sb("bqc", [128, 1])
        g12 = sb("g12", [128, 1])
        b12 = sb("b12", [128, 1])
        eps = sb("eps", [128, 1])
        wm = sb("wm", [128, D + 1])
        gw = sb("gw", [128, D])
        wtmp = sb("wtmp", [128, D])
        brow = sb("brow", [P, D + 1])
        v3 = sb("v3", [128, 4, D])
        bfb = sb("bfb", [P, 1])
        k0 = sb("k0", [P, 2])
        blockones = sb("blockones", [128, 128])
        X = [[sb(f"X{q}{b}", [128, BLK]) for b in range(NB)] for q in range(2)]
        SQ = [sb(f"SQ{b}", [128, BLK]) for b in range(NB)]
        ZB = [sb(f"ZB{b}", [P, TB, D + 1]) for b in range(NB)]
        ZQ = [sb(f"ZQ{b}", [P, TB, D]) for b in range(NB)]
        var3 = sb("var3", [P, COLS])
        num3 = sb("num3", [P, COLS])

        bank = [ctx.enter_context(nc.psum_tensor(f"bank{k}", [128, 512], f32)) for k in range(8)]
        psA = [[bank[2 * q + b] for b in range(NB)] for q in range(2)]
        acc = [bank[4], bank[5]]
        psCV, psZ = bank[6], bank[7]
        psT, psX, psO, psS, psB = [bank[0], bank[1]], [bank[2], bank[3]], [bank[4], bank[5]], bank[6], bank[7]

        s_ends, s_cate, s_cont, s_par, s_tabT = sem("ends_loaded"), sem("cate_loaded"), sem("cont_loaded"), sem("params_loaded"), sem("tabT_loaded")
        s_w4, s_first = sem("w4_loaded"), sem("wc_bc_loaded")
        s_nch = [sem(f"nodes_loaded{k}") for k in range(2)]
        s_iota, s_dve, s_id = sem("iotas_ready"), sem("dve_chain"), sem("ident_ready")
        s_xt, s_xs, s_xo = sem("nodes_transposed"), sem("nodesT_copied"), sem("nodes_projected")
        s_cmax, s_call, s_nr = sem("counts_ready"), sem("counts_reduced"), sem("rounds_ready")
        s_cateh, s_cxp, s_store = sem("cate16_ready"), sem("features_part_ready"), sem("scratch_stored")
        s_bs, s_bt, s_bsq, s_sqs, s_bv = sem("bn_sums"), sem("bn_totals"), sem("bn_centred"), sem("bn_squares"), sem("bn_sqrt")
        s_wc, s_tps, s_tev = sem("wc_ready"), sem("T_product"), sem("T_copied")
        s_tmax, s_tall, s_bqp, s_bqd = sem("tmax_ready"), sem("tmax_reduced"), sem("bq_ready"), sem("bq_column")
        s_prep, s_ready = sem("setup_done"), sem("graph_constants_ready")
        passes = ["deg"] + [f"l{l}" for l in range(LAYERS)]
        s_slotd = {k: sem(f"slotd_ready_{k}") for k in passes}
        s_slotp = [sem(f"slot_ready{l}") for l in range(LAYERS)]
        s_gath = {k: [sem(f"gathered_{k}{h}") for h in range(2)] for k in passes[1:]}
        s_lo8 = {k: sem(f"lo8_ready_{k}") for k in passes}
        s_hi = {k: sem(f"hi_ready_{k}") for k in passes}
        s_lo = {k: sem(f"lo_ready_{k}") for k in passes[1:]}
        s_ohu = {k: sem(f"onehots_used_{k}") for k in passes}
        s_ext = sem("pack_chain")
        s_pass, s_accz = sem("pass_done"), sem("acc_read")
        s_degm, s_degs = sem("deg_ready"), sem("deg_sqrt")
        s_umax, s_uall, s_utab, s_ust = sem("umax_ready"), sem("umax_reduced"), sem("utab_ready"), sem("utab_stored")
        s_outt, s_outst, s_dl, s_ydf, s_ydst = sem("out_ready"), sem("out_stored"), sem("dlast_loaded"), sem("yd_filled"), sem("yd_stored")
        s_dslot, s_dsc, s_ydl = sem("dst_slots_ready"), [sem("d_scattered0"), sem("d_scattered1")], sem("yd_loaded")
        s_dg = [sem("d_gathered0"), sem("d_gathered1")]
        s_sslot, s_sg, s_sout = sem("src_slots_ready"), [sem("s_gathered0"), sem("s_gathered1")], sem("ys_copied")
        s_own = {e: sem(f"carries_waits_{e}") for e in ("dve", "pool", "sp", "pe")}
        t_cate = [sem(f"t_cate_loaded{q}") for q in range(2)]
        t_cx = [sem(f"t_cx_loaded{q}") for q in range(2)]
        t_ci = [sem(f"t_cate_tiles_loaded{q}") for q in range(2)]
        t_rows = [sem(f"t_T_rows_gathered{g}") for g in range(len(CATS))]
        t_rowsfree = [sem(f"t_T_rows_used{g}") for g in range(len(CATS))]
        s_t16, s_t16st = sem("T16_ready"), sem("T16_stored")
        t_cm = sem("t_cate_shifted")
        t_oh, t_ohfree = sem("t_onehot_ready"), sem("t_onehot_free")
        t_A, t_Afree = sem("t_A_done"), sem("t_A_evacuated")
        t_C, t_Cfree = sem("t_C_done"), sem("t_C_evacuated")
        t_lo, t_x = sem("t_lo_copied"), sem("t_x_ready")
        t_sq, t_V, t_ln, t_sd = sem("t_square_ready"), sem("t_V_done"), sem("t_ln_ready"), sem("t_sd_ready")
        t_xn, t_R = sem("t_xn_ready"), sem("t_R_ready")
        t_Z, t_zb, t_zq, t_red = sem("t_Z_done"), sem("t_zb_ready"), sem("t_zq_ready"), sem("t_zq_reduced")
        s_fin, s_fs, s_y, s_out = sem("fin_var"), sem("fin_rstd"), sem("y_ready"), sem("y_stored")
        primed = [*t_rowsfree, t_x, t_V, t_ln, t_sd, t_xn, t_Z, t_zb, t_zq, t_red, t_Cfree, t_R, s_ext]
        BACK = TOP + PRIME

        block = ctx.enter_context(nc.Block())

        def rows(v, n, parts):
            return v.rearrange("(o c) -> o c", o=1).broadcast_to([parts, n])

        NPAR = 15
        PASS_SB = RS + 2
        TAIL = 1 + len(passes) * PASS_SB

        def schedule(eng, body, between, middle=None):
            used = [0] * len(CATS)

            def pair(it, i, sets, what=({}, {})):
                per = [sum(g in s for s in sets) for g in range(len(CATS))]
                for k in range(2):
                    cats = [(g, it * per[g] + (used[g] + (k if g in sets[0] else 0))) for g in sets[k]]
                    body(2 * it + (i + k), (i + k) % 2, it + (i + k) // 2, cats=cats, **what[k])
                return per

            def pairs(n, i, sets, what=lambda it: ({}, {})):
                with eng.Fori(0, n) as it:
                    per = pair(it, i, sets, what(it))
                for g in range(len(CATS)):
                    used[g] += n * per[g]

            body(0, 0, 0, prev=False)
            for n in range(len(passes)):
                i0 = 1 + n * PASS_SB
                pairs(RS // 2, i0, GATHERED["layer" if n else "deg"], lambda it: (dict(graph=(n, 2 * it)), dict(graph=(n, 2 * it + 1))))
                between(n)
                per = pair(0, i0 + RS, GATHERED["nodes"], (dict(nodes=n), {}))
                used = [a + b for a, b in zip(used, per)]
            if middle:
                middle()
            else:
                pairs((NSB - TAIL) // 2 - TAIL_PAIRS, TAIL, ((), ()))
            pairs(TAIL_PAIRS - 1, NSB - 2 * TAIL_PAIRS, GATHERED["tail"])
            pair(0, NSB - 2, GATHERED["tail"], ({}, dict(last=True)))

        def one_hot_steps(cats):
            left = [c for c in range(CATE) if c not in [CATS[g] for g, _ in cats]]
            n = len(left) * KT
            for v in range(NKT):
                kt = v * n // NKT
                new = v == 0 or kt != (v - 1) * n // NKT
                yield (v, kt if new else None, left[kt // KT], kt % KT)

        def skipped(cats):
            return len(cats) * KT

        @block.sync
        def _(sp):
            sp.dma_start(wc[:, :, :], Wc.rearrange("d (c k) -> d c k", c=CATE)).then_inc(s_first, 16)
            sp.dma_start(bcb[:, :], rows(bc, D, P)).then_inc(s_first, 16)
            sp.dma_start(tabT, tableT).then_inc(s_tabT, 16)
            sp.dma_start(cate_i, cate).then_inc(s_cate, 16)
            sp.dma_start(cont_f, cont.rearrange("s (c k) -> s c k", c=CONT)).then_inc(s_cont, 16)

            def par(dst, src):
                sp.dma_start(dst, src).then_inc(s_par, 16)

            par(bnp[:, 0, :], rows(bn_g, CONT, P))
            par(bnp[:, 1, :], rows(bn_b, CONT, P))
            par(wq6[:, :], Wq6)
            par(pmask[:, :], partmask)
            par(bqr[:, :], rows(bq, D, 1))
            for k, (g, b) in enumerate(((ln1_g, ln1_b), (ln2_g, ln2_b))):
                par(g12[D * k:D * k + D, :], g.rearrange("(c o) -> c o", o=1))
                par(b12[D * k:D * k + D, :], b.rearrange("(c o) -> c o", o=1))
            par(wm[:, 0:D], Wm)
            for k, v in enumerate((ln3_g, ln3_b, Wf[2 * D:3 * D], bm)):
                par(v3[:, k, :], rows(v, D, 128))
            par(bfb[:, :], rows(bf, 1, P))
            sp.wait_ge(s_cateh, 1)
            sp.dma_start(cate16_d, cate_h).then_inc(s_store, 16)
            sp.wait_ge(s_t16, 1)
            for k, c in enumerate(CATS):
                sp.dma_start(T16_d[k].rearrange("(j p) k -> p j k", p=P), T16[:, :, c, :]).then_inc(s_t16st, 16)
            for k in range(3):
                sp.wait_ge(s_cxp, k + 1)
                sp.dma_start(cxp_d[k].rearrange("s (c k) -> s c k", c=CONT), cont_part).then_inc(s_store, 16)

            def load(i, q):
                sp.dma_start(cate_b[q],
                             cate16_d[ds(i, 1), :].broadcast_to([P, CATE * SB]).rearrange("p (c k) -> p c k", c=CATE)).then_inc(t_cate[q], 16)
                for g, (a, _) in enumerate(XPARTS):
                    sp.dma_start(cx[q][g * CONT:(g + 1) * CONT, :],
                                 cxp_d[a][ds(i, 1), :].rearrange("o (c k) -> (o c) k", c=CONT)).then_inc(t_cx[q], 16)

            def load_tiles(i, q):
                sp.dma_start(slot_c[q][:, :, :], cate_tiles[ds(i, 1), :, :].rearrange("o p (c t) -> (o p) c t", c=CATE)[:, CATE - len(CATS):CATE, :]).then_inc(t_ci[q], 16)

            sp.wait_ge(s_prep, 1)
            load(0, 0)
            load(1, 1)
            load_tiles(1, 1)

            def body(i, q, u, cats=(), prev=True, graph=None, nodes=None, last=False):
                if not prev or last:
                    return
                sp.wait_ge(t_oh, i * NKT)
                sp.sem_inc(s_own["sp"], 1)
                sp.wait_ge(t_C, i * NB)
                sp.sem_inc(s_own["sp"], 1)
                load(i + 1, 1 - q)
                sp.wait_ge(t_ohfree, i * NKT + RING)
                sp.sem_inc(s_own["sp"], 1)
                load_tiles(i + 1, 1 - q)

            schedule(sp, body, lambda n: None)
            sp.wait_ge(s_y, 1)
            sp.dma_start(y, ys[:, :]).then_inc(s_out, 16)
            sp.wait_ge(s_out, 16)

        @block.gpsimd
        def _(pool):
            G = nc.gpsimd
            G.iota(pidx_i[:, :], pattern=[[0, 1]], base=0, channel_multiplier=1).then_inc(s_iota, 1)
            G.iota(iota_i[:, :, :], pattern=[[0, 2], [1, HALF]], base=0, channel_multiplier=0).then_inc(s_iota, 1)
            G.iota(ebase_i[:, :], pattern=[[HALF, 2], [0, TOP]], base=HALF - HALF + 256, channel_multiplier=COLS).then_inc(s_iota, 1)
            G.memset(ident[:, :], 0.0).then_inc(s_id, 1)
            pool.wait_ge(s_id, 1)
            G.affine_select(out=ident[:, :], in_=ident[:, :], compare_op=ALU.not_equal, fill=1.0, base=0,
                            pattern=[[-1, P]], channel_multiplier=1).then_inc(s_id, 1)
            pool.wait_ge(s_tmax, 1)
            G.partition_all_reduce(tmax[:, 1:2], tmax[:, 0:1], 128, RMAX).then_inc(s_tall, 1)
            pool.wait_ge(s_cmax, 1)
            G.partition_all_reduce(call[:, :], cmax[:, :], P, RMAX).then_inc(s_call, 1)
            pool.wait_ge(s_nr, 1)
            rounds = pool.value_load(nround[0:1, 1:2], min_val=RS, max_val=ROUNDS_MAX)

            def gather(out, table, index, done):
                G.indirect_dma_start(out=out, out_offset=None, in_=table,
                                     in_offset=bass.IndirectOffsetOnAxis(index, 0)).then_inc(done, 16)

            def table(l):
                pool.wait_ge(s_umax, l + 1)
                G.partition_all_reduce(umax[:, 1:2], umax[:, 0:1], P, RMAX).then_inc(s_uall, 1)
                pool.wait_ge(s_utab, l + 1)
                pool.dma_start(u_d[l].rearrange("(p h) k -> p h k", p=P), utab).then_inc(s_ust, 16)
                pool.wait_ge(s_ust, 16 * (l + 1))

            def graph_half(n, r, h):
                k = passes[n]
                pool.wait_ge(s_lo[k], r * ROUND + (h * TOP + PRIME))
                pool.sem_inc(s_own["pool"], 1)
                G.tensor_copy(slot[h][:, :], packed[:, 0, ds(r * ROUND + h * TOP, TOP)]).then_inc(s_slotp[n - 1], 1)
                pool.wait_ge(s_slotp[n - 1], 2 * r + (h + 1))
                pool.sem_inc(s_own["pool"], 1)
                for t in range(TOP):
                    gather(gath[h][:, t, :], u_d[n - 1], slot[h][:, t:t + 1], s_gath[k][h])

            def rows_of(g, used, q, u):
                pool.wait_ge(t_ci[q], (u + (1 if q else 0)) * 16)
                pool.wait_ge(t_rowsfree[g], used + PRIME)
                pool.sem_inc(s_own["pool"], 1)
                for t in range(TILES):
                    gather(rowsT[g][:, t, :], T16_d[g], slot_c[q][:, LOADED.index(CATS[g]), t:t + 1], t_rows[g])

            def body(i, q, u, cats=(), prev=True, graph=None, nodes=None, last=False):
                ways = [lambda g=g, used=used: rows_of(g, used, q, u) for g, used in cats]
                if graph and graph[0]:
                    graph_half(graph[0], graph[1], 0)
                for w in ways[:1]:
                    w()
                if graph and graph[0]:
                    graph_half(graph[0], graph[1], 1)
                if nodes is not None and nodes < LAYERS:
                    table(nodes)
                for w in ways[1:]:
                    w()

            def between(n):
                if n:
                    with pool.If(rounds > RS):
                        with pool.Fori(RS, rounds) as r:
                            for h in range(2):
                                graph_half(n, r, h)

            def out_gathers():
                pool.wait_ge(s_outt, 1)
                pool.dma_start(out_d.rearrange("(p h) k -> p h k", p=P), otab).then_inc(s_outst, 16)
                pool.wait_ge(s_outst, 16)
                pool.dma_start(dlast[:, :], out_d[N - 1:N, 1:2].broadcast_to([P, 1])).then_inc(s_dl, 16)
                G.memset(yd[:, :], 0.0).then_inc(s_ydf, 1)
                pool.wait_ge(s_dl, 16)
                pool.wait_ge(s_ydf, 1)
                G.tensor_scalar(yd[:, :], yd[:, :], dlast[:, 0:1], None, ALU.add).then_inc(s_ydf, 1)
                pool.wait_ge(s_ydf, 2)
                pool.dma_start(yd_d.rearrange("(p c) o -> p (c o)", p=P), yd[:, :]).then_inc(s_ydst, 16)
                pool.wait_ge(s_ydst, 16)
                def dst_round(r, first):
                    for h in range(2):
                        if not first:
                            pool.wait_ge(s_dsc[h], r * (16 * TOP))
                            pool.sem_inc(s_own["pool"], 1)
                        G.tensor_copy(slot_d2[h][:, :, :], packed[:, 1:3, ds(r * ROUND + h * TOP, TOP)]).then_inc(s_dslot, 1)
                        pool.wait_ge(s_dslot, 2 * r + (h + 1))
                        pool.sem_inc(s_own["pool"], 1)
                        for t in range(TOP):
                            gather(gd[h][:, t, :], out_d, slot_d2[h][:, 0, t:t + 1], s_dg[h])
                    for h in range(2):
                        pool.wait_ge(s_dg[h], r * (16 * TOP) + 16 * TOP)
                        pool.sem_inc(s_own["pool"], 1)
                        for t in range(TOP):
                            G.indirect_dma_start(out=yd_d, out_offset=bass.IndirectOffsetOnAxis(slot_d2[h][:, 1, t:t + 1], 0),
                                                 in_=gd[h][:, t, 1:2], in_offset=None,
                                                 bounds_check=E - 1, oob_is_err=False).then_inc(s_dsc[h], 16)

                dst_round(0, True)
                with pool.Fori(1, rounds) as r:
                    dst_round(r, False)
                for h in range(2):
                    pool.wait_ge(s_dsc[h], rounds * (16 * TOP))
                    pool.sem_inc(s_own["pool"], 1)
                pool.dma_start(yd[:, :], yd_d.rearrange("(p c) o -> p (c o)", p=P)).then_inc(s_ydl, 16)

                def src_step(c, q, first):
                    if not first:
                        src_out(c, q)
                    G.tensor_copy(slot_s[q][:, :], ends[:, 0, ds(c * GSTEP, GSTEP)]).then_inc(s_sslot, 1)
                    pool.wait_ge(s_sslot, c + 1)
                    pool.sem_inc(s_own["pool"], 1)
                    for t in range(GSTEP):
                        gather(gs[q][:, t, :], out_d, slot_s[q][:, t:t + 1], s_sg[q])

                def src_out(c, q):
                    pool.wait_ge(s_sg[q], (c - q) * (8 * GSTEP))
                    pool.sem_inc(s_own["pool"], 1)
                    G.tensor_copy(ys[:, ds((c - 2) * GSTEP, GSTEP)], gs[q][:, :, 0]).then_inc(s_sout, 1)
                    pool.wait_ge(s_sout, c - 1)
                    pool.sem_inc(s_own["pool"], 1)

                NSTEP = COLS // GSTEP
                src_step(0, 0, True)
                src_step(1, 1, True)
                with pool.Fori(1, NSTEP // 2) as it:
                    src_step(2 * it, 0, False)
                    src_step(2 * it + 1, 1, False)
                src_out(NSTEP, 0)
                src_out(NSTEP + 1, 1)

            pool.wait_ge(s_t16st, 16 * len(CATS))
            schedule(pool, body, between, middle=out_gathers)

        @block.tensor
        def _(pe):
            mm = nc.tensor.matmul
            pe.wait_ge(s_wc, 1)
            pe.wait_ge(s_tabT, 16)
            for j in range(KT):
                if j >= 2:
                    pe.wait_ge(s_tev, j - 1)
                mm(psT[j % 2][0:P, 0:CATE * D], lhsT=tabT[:, j * P:(j + 1) * P], rhs=wc[:, :, :].rearrange("d c k -> d (c k)"),
                   start=True, stop=True).then_inc(s_tps, 1)

            pe.wait_ge(s_id, 2)
            pe.wait_ge(s_w4, 65)
            groups = [(c, g) for c in range(NCH) for g in range(0, CH // 2, 4)]

            def project(m):
                c, g = groups[m]
                pe.wait_ge(s_xs, m + 1)
                for t in range(min(4, CH // 2 - g)):
                    hi2 = c * CH + 2 * (g + t)
                    o = psO[hi2 * 2 // 500]
                    last = mm(o[0:P, hi2 * 2 % 500:hi2 * 2 % 500 + 4], lhsT=xT[m % 2][:, t * P:(t + 1) * P], rhs=w4[:, :],
                              start=True, stop=True, skip_group_check=True)
                last.then_inc(s_xo, 1)

            def bn_total(k):
                pe.wait_ge(s_bs, k + 1)
                mm(psS[0:P, 8 * k:8 * k + CONT], lhsT=onesm[:, :], rhs=bstat[:, k, :], start=True, stop=True).then_inc(s_bt, 1)

            for m, (c, g) in enumerate(groups):
                if (c, g) == (BN_CHUNKS[0], 0):
                    bn_total(0)
                if (c, g) == (BN_CHUNKS[1], 0):
                    bn_total(1)
                    pe.wait_ge(s_bqp, 1)
                    mm(psB[D:2 * D, 0:1], lhsT=bqr[:, :], rhs=one1[:, :], start=True, stop=True).then_inc(s_bqd, 1)
                if g == 0:
                    pe.wait_ge(s_nch[c % 2], 16 * (c // 2 + 1))
                if m >= 2:
                    pe.wait_ge(s_xs, m - 1)
                for t in range(min(4, CH // 2 - g)):
                    last = nc.tensor.transpose(psX[m % 2][0:128, t * P:(t + 1) * P],
                                               nchunk[c % 2][:, 2 * (g + t):2 * (g + t) + 2, :].rearrange("p h d -> p (h d)"), ident[:, :])
                last.then_inc(s_xt, 1)
                if m:
                    project(m - 1)
            project(len(groups) - 1)

            pe.wait_ge(s_ready, 1)
            pe.wait_ge(s_nr, 1)
            rounds = pe.value_load(nround[0:1, 0:1], min_val=1, max_val=ROUNDS_MAX)
            pe.wait_ge(s_prep, 1)

            def zero_product(c, start):
                return mm(acc[c][0:P, 0:HI], lhsT=zero_l[:, :], rhs=iota16[:, :], start=start, stop=not start,
                          skip_group_check=True)

            def pass_start(n):
                if n:
                    pe.wait_ge(s_accz, n)
                for c in range(2):
                    zero_product(c, True)

            def graph_tile(n, r, t):
                k = passes[n]
                pe.wait_ge(s_hi[k], r * ROUND + (t + 1 + PRIME))
                if n:
                    pe.wait_ge(s_lo[k], r * ROUND + (t + 1 + BACK))
                    for v in range(4):
                        last = mm(acc[v % 2][0:P, 0:HI], lhsT=oh_lo[t % GR][:, v, :], rhs=oh_hi[t % GR][:, :],
                                  start=False, stop=False, skip_group_check=True)
                else:
                    last = mm(acc[0][0:P, 0:HI], lhsT=oh_lo8[t // TOP][:, t % TOP, :], rhs=oh_hi[t % GR][:, :],
                              start=False, stop=False, skip_group_check=True)
                last.then_inc(s_ohu[k], 1)

            def gathered_rows(q, g, used):
                pe.wait_ge(t_rows[g], used * (16 * TILES) + 16 * TILES)
                for t in range(TILES):
                    b, at = t // TB, t % TB * P
                    last = mm(psA[q][b][:, at:at + P], lhsT=rowsT[g][:, t, :], rhs=ident16[:, :], start=False, stop=False,
                              skip_group_check=True)
                last.then_inc(t_rowsfree[g], 1)

            def feature_product(i, q, u, b, prev):
                if b == 0:
                    pe.wait_ge(t_cx[q], (u + 1) * (16 * len(XPARTS)))
                    if prev:
                        pe.wait_ge(t_ln, i * NB + PRIME)
                else:
                    pe.wait_ge(t_Cfree, i * NB + (b + PRIME))
                pe.sem_inc(s_own["pe"], 1)
                mm(psCV[D:2 * D, 0:BLK], lhsT=wqx[:, :], rhs=cx[q][:, b * BLK:(b + 1) * BLK],
                   start=True, stop=True).then_inc(t_C, 1)

            def variances(i, b):
                pe.wait_ge(t_sq, i * NB + (b + 1))
                if b == 0:
                    pe.wait_ge(t_Cfree, i * NB + (NB + PRIME))
                else:
                    pe.wait_ge(t_ln, i * NB + (b + PRIME))
                mm(psCV[:, 0:BLK], lhsT=blockones[:, :], rhs=SQ[b][:, :], start=True, stop=True).then_inc(t_V, 1)

            def last_product(i, b):
                pe.wait_ge(t_R, i * NB + (b + 1 + PRIME))
                pe.wait_ge(t_zb, i * NB + (b + PRIME))
                for t in range(TB):
                    last = mm(psZ[0:P, t * (D + 1):(t + 1) * (D + 1)], lhsT=R[b][:, t * P:(t + 1) * P], rhs=wm[:, :],
                              start=True, stop=True, skip_group_check=True)
                last.then_inc(t_Z, 1)

            def body(i, q, u, cats=(), prev=True, graph=None, nodes=None, last=False):
                if not prev:
                    pass_start(0)
                count = NKT - skipped(cats)
                for v, kt, c, j in one_hot_steps(cats):
                    if kt is not None:
                        pe.wait_ge(t_oh, i * NKT + (kt + 1))
                        for b in range(NB):
                            if kt == 0:
                                pe.wait_ge(t_Afree, i * NB + (b + 1))
                            ins = mm(psA[q][b][:, 0:BLK], lhsT=T16[:, j, c, :], rhs=onehot[kt % RING][:, b * BLK:(b + 1) * BLK],
                                     start=kt == 0, stop=kt == count - 1, skip_group_check=True)
                            if kt == count - 1 and b == 0:
                                ins.then_inc(t_A, 1)
                        ins.then_inc(t_ohfree, 1 if kt else 1 + skipped(cats))
                    for g, used in cats:
                        if v == AT_CATS[g]:
                            gathered_rows(q, g, used)
                    if graph and v in AT_TILE:
                        graph_tile(graph[0], graph[1], AT_TILE.index(v))
                    if prev and v in AT_PE["variance"]:
                        variances(i - 1, AT_PE["variance"].index(v))
                    if v in AT_PE["feature"]:
                        feature_product(i, q, u, AT_PE["feature"].index(v), prev)
                    if prev and v in AT_PE["product"]:
                        last_product(i - 1, AT_PE["product"].index(v))

            def between(n):
                with pe.If(rounds > RS):
                    with pe.Fori(RS, rounds) as r:
                        for t in range(ROUND):
                            graph_tile(n, r, t)
                for c in range(2):
                    ins = zero_product(c, False)
                ins.then_inc(s_pass, 1)
                if n + 1 < len(passes):
                    pass_start(n + 1)

            schedule(pe, body, between)
            for b in range(NB):
                variances(NSB - 1, b)
            for b in range(NB):
                last_product(NSB - 1, b)

        @block.scalar
        def _(act):
            A = nc.scalar.activation
            act.dma_start(ends[:, 0, :], src_e).then_inc(s_ends, 16)
            act.dma_start(ends[:, 1, :], dst_e).then_inc(s_ends, 16)
            act.wait_ge(s_w4, 1)
            for k in range(2):
                for c in range(2):
                    act.dma_start(w4[D * k:D * k + D, 2 * k + c:2 * k + c + 1],
                                  Wf[c * D:(c + 1) * D].rearrange("(d o) -> d o", o=1)).then_inc(s_w4, 16)
            for c in range(2):
                act.dma_start(nchunk[c], node_emb[:, c * CH * D:(c + 1) * CH * D].rearrange("p (c d) -> p c d", d=D)).then_inc(s_nch[c], 16)
            per = -(-(CH // 2) // 4)
            for m in range(NCH * per):
                c, g = m // per, m % per
                w = min(4, CH // 2 - 4 * g) * P
                if (c, g) == (BN_CHUNKS[0] + 1, 0):
                    for f in range(CONT):
                        act.wait_ge(s_bsq, f + 1)
                        if f:
                            act.wait_ge(s_sqs, f)
                        A(sqj[:, :], cont_f[:, f, :], ACT.Square, accum_out=bstat[:, 1, f:f + 1]).then_inc(s_sqs, 1)
                act.wait_ge(s_xt, m + 1)
                if m >= 2:
                    act.wait_ge(s_xo, m - 1)
                A(xT[m % 2][:, 0:w], psX[m % 2][:, 0:w], ACT.Copy).then_inc(s_xs, 1)
                if g == per - 1 and c + 2 < NCH:
                    act.dma_start(nchunk[c % 2], node_emb[:, (c + 2) * CH * D:(c + 3) * CH * D].rearrange("p (c d) -> p c d", d=D)).then_inc(s_nch[c % 2], 16)
                if (c, g) == (BN_CHUNKS[1], per - 1):
                    act.wait_ge(s_bv, 1)
                    A(bstat[:, 3, :], bstat[:, 2, :], ACT.Sqrt).then_inc(s_bv, 1)
            nc.scalar.preload_act_table_set("natural_log_exp_and_others")
            act.wait_ge(s_nr, 1)
            rounds = act.value_load(nround[0:1, 0:1], min_val=1, max_val=ROUNDS_MAX)
            act.wait_ge(s_prep, 1)

            def feature_evac(i, q, b, prev=True):
                act.wait_ge(t_C, i * NB + (b + 1))
                if prev:
                    act.wait_ge(t_xn, (i - 1) * NB + PRIME)
                A(X[q][b][D:2 * D, :], psCV[D:2 * D, 0:BLK], ACT.Identity, bias=bqc[D:2 * D, :]).then_inc(t_Cfree, 1)

            def lo_copy(i, q, b):
                if b == 0:
                    act.wait_ge(t_A, i + 1)
                else:
                    act.wait_ge(t_ohfree, i * NKT + (NKT + RING))
                act.wait_ge(t_x, i * NB + PRIME)
                A(lo_part[b], psA[q][b][D:2 * D, 0:BLK], ACT.Copy, scale=sc_i[0:D, 0:1].bitcast(f32)).then_inc(t_lo, 1)

            def square(i, q, b):
                act.wait_ge(t_x, i * NB + (b + 1 + PRIME))
                act.wait_ge(t_Cfree, i * NB + (b + 1 + PRIME))
                act.wait_ge(t_V, i * NB + PRIME)
                A(SQ[b][:, :], X[q][b][:, :], ACT.Square).then_inc(t_sq, 1)

            def rstd(i, b):
                act.wait_ge(t_V, i * NB + (b + 1 + PRIME))
                act.wait_ge(t_R, i * NB + PRIME)
                A(SD[b], psCV[:, 0:BLK], ACT.Ln, bias=eps[:, :]).then_inc(t_ln, 1)
                act.wait_ge(t_ln, i * NB + (b + 1 + PRIME))
                A(SD[b], SD[b], ACT.Exp, scale=-0.5).then_inc(t_sd, 1)

            def relu(i, b):
                act.wait_ge(t_xn, i * NB + (b + 1 + PRIME))
                act.wait_ge(t_Z, i * NB + PRIME)
                A(R[b], SD[b], ACT.Relu, scale=g12[:, :], bias=b12[:, :]).then_inc(t_R, 1)

            def last_square(i, b):
                act.wait_ge(t_zb, i * NB + (b + 1 + PRIME))
                act.wait_ge(t_red, i * NB + PRIME)
                A(ZQ[b][:, :, :], ZB[b][:, :, 0:D], ACT.Square).then_inc(t_zq, 1)

            def graph_tile(n, r, t):
                k = passes[n]
                h = t // TOP
                if t % TOP == 0:
                    act.wait_ge(s_gath[k][h], r * (16 * TOP) + 16 * TOP)
                    act.wait_ge(s_lo8[k], 2 * r + (h + 1))
                act.wait_ge(s_ohu[k], r * ROUND + (t + 1))
                for v in range(4):
                    ins = A(oh_lo[t % GR][:, v, :], oh_lo8[h][:, t % TOP, :], ACT.Copy, scale=gath[h][:, t % TOP, v:v + 1])
                ins.then_inc(s_lo[k], 1)

            def body(i, q, u, cats=(), prev=True, graph=None, nodes=None, last=False):
                if not prev:
                    feature_evac(i, q, 0, False)
                    feature_evac(i, q, 1, False)
                    return
                j, p = i - 1, 1 - q
                step = dict(lo=lambda b: lo_copy(j, p, b), square=lambda b: square(j, p, b), rstd=lambda b: rstd(j, b),
                            relu=lambda b: relu(j, b), feature=lambda b: feature_evac(i, q, b), zsquare=lambda b: last_square(j, b))
                for kt in range(NKT):
                    for what, at in AT_ACT.items():
                        if kt in at:
                            step[what](at.index(kt))
                    if graph and graph[0]:
                        for t in range(ROUND):
                            if max(AT_TILE[t] - ACT_LEAD, 0) == kt:
                                graph_tile(graph[0], graph[1], t)
                    if nodes == 0 and kt == 8:
                        act.wait_ge(s_degm, 1)
                        A(degm[:, :], degm[:, :], ACT.Sqrt).then_inc(s_degs, 1)
                        nc.scalar.preload_act_table_set("natural_log_exp_and_others")

            def between(n):
                if n:
                    with act.If(rounds > RS):
                        with act.Fori(RS, rounds) as r:
                            for t in range(ROUND):
                                graph_tile(n, r, t)

            schedule(act, body, between)
            i, q = NSB - 1, (NSB - 1) % 2
            for step in (lambda b: lo_copy(i, q, b), lambda b: square(i, q, b), lambda b: rstd(i, b), lambda b: relu(i, b),
                         lambda b: last_square(i, b)):
                for b in range(NB):
                    step(b)
            act.wait_ge(s_fin, 1)
            A(var3[:, :], var3[:, :], ACT.Ln, scale=1.0 / D, bias=eps[0:P, :]).then_inc(s_fs, 1)
            act.wait_ge(s_fs, 1)
            A(var3[:, :], var3[:, :], ACT.Exp, scale=-0.5).then_inc(s_fs, 1)

        @block.vector
        def _(dve):
            V = nc.vector
            chain = [0]

            def link(ins):
                chain[0] += 1
                ins.then_inc(s_dve, 1)
                dve.wait_ge(s_dve, chain[0])

            V.memset(w4[:, :], 0.0).then_inc(s_w4, 1)
            V.memset(onesm[:, :], 1.0)
            for x in primed:
                dve.sem_inc(x, PRIME)
            dve.sem_inc(t_ohfree, RING)
            dve.sem_inc(t_Afree, 2 * NB)
            for k in passes:
                dve.sem_inc(s_ohu[k], GR)
                dve.sem_inc(s_hi[k], PRIME)
            for k in passes[1:]:
                dve.sem_inc(s_lo[k], BACK)

            def centre(w, parts, n):
                m = wsum[0:parts, 0:1]
                link(V.tensor_reduce(m, w, AX.X, ALU.add))
                link(V.tensor_scalar(m, m, 1.0 / n, None, ALU.mult))
                link(V.tensor_scalar(w, w, m, None, ALU.subtract))

            def power_scale(bits, top):
                link(V.tensor_scalar(bits[:, 0:1], top.bitcast(i32), 0x7F800000, None, ALU.bitwise_and))
                link(V.tensor_scalar(bits[:, 0:1], bits[:, 0:1], -float(F_MAX * 2 ** 23), float(2 ** 23), ALU.add, ALU.max))
                link(V.tensor_scalar(bits[:, 1:2], bits[:, 0:1], -1.0, 254.0 * 2 ** 23, ALU.mult, ALU.add))

            dve.wait_ge(s_first, 32)
            m5 = wsum[0:D, 0:CATE]
            link(V.tensor_reduce(m5, wc[:, :, :], AX.X, ALU.add))
            link(V.tensor_scalar(m5, m5, 1.0 / D, None, ALU.mult))
            link(V.tensor_tensor(wc[:, :, :], wc[:, :, :],
                                 m5.rearrange("p (c o) -> p c o", o=1).broadcast_to([D, CATE, D]), ALU.subtract))
            dve.sem_inc(s_wc, 1)
            centre(bcb[:, :], P, D)
            link(V.memset(tmax[:, :], 0.0))
            for j in range(KT):
                dve.wait_ge(s_tps, j + 1)
                V.tensor_copy(Tf[:, j, :, :], psT[j % 2][0:P, 0:CATE * D].rearrange("p (c d) -> p c d", c=CATE)).then_inc(s_tev, 1)
            dve.wait_ge(s_tev, KT)
            link(V.memset(Tf[0:1, 0, :, :], 0.0))
            link(V.tensor_tensor(Tf[:, :, 0, :], Tf[:, :, 0, :],
                                 bcb[:, :].rearrange("p (o d) -> p o d", o=1).broadcast_to([P, KT, D]), ALU.add))
            V.tensor_reduce(tmax[0:P, 0:1], Tf, AX.XYZ, ALU.max, apply_absolute_value=True).then_inc(s_tmax, 1)
            dve.wait_ge(s_cate, 16)
            V.tensor_copy(cate_h, cate_i).then_inc(s_cateh, 1)
            dve.wait_ge(s_tall, 1)
            power_scale(sc_i, tmax[:, 1:2])
            Tv = Tf.rearrange("p j c d -> p (j c) d")
            T16v = T16[:, :, :, :].rearrange("p j c d -> p (j c) d")
            link(V.tensor_scalar(Tv, Tv, sc_i[0:P, 1:2].bitcast(f32), None, ALU.mult))
            link(V.tensor_copy(T16v[:, :, 0:D], Tv))
            link(V.tensor_tensor(T16v[:, :, D:2 * D], Tv, T16v[:, :, 0:D], ALU.subtract))
            dve.sem_inc(s_t16, 1)
            dve.wait_ge(s_id, 2)
            V.tensor_copy(ident16[:, :], ident[:, :])
            dve.wait_ge(s_cont, 16)
            V.tensor_reduce(bstat[:, 0, :], cont_f, AX.X, ALU.add).then_inc(s_bs, 1)
            dve.wait_ge(s_bt, 1)
            link(V.tensor_scalar(bstat[:, 0, :], psS[0:P, 0:CONT], 1.0 / E, None, ALU.mult))
            for c in range(CONT):
                V.tensor_scalar(cont_f[:, c, :], cont_f[:, c, :], bstat[:, 0, c:c + 1], None, ALU.subtract).then_inc(s_bsq, 1)

            dve.wait_ge(s_iota, 3)
            V.tensor_copy(pidx[:, :], pidx_i[:, :])
            V.tensor_copy(iota16[:, :], iota_i[:, 0, :])
            V.tensor_copy(ebase[:, :], ebase_i[:, :])
            link(V.memset(zero_l[:, :], 0.0))
            dve.sem_inc(s_ready, 1)
            link(V.tensor_scalar(col_key, iota_i[:, :, :], -256.0, 65536.0, ALU.add, ALU.mult))
            dve.wait_ge(s_ends, 32)
            link(V.tensor_copy(dst_f, ends[:, 1, :]))
            link(V.tensor_scalar(valid, dst_f, float(N), None, ALU.is_lt))
            link(V.tensor_reduce(cnt[:, :], valid.rearrange("p (h c) -> p h c", h=2), AX.X, ALU.add))
            V.tensor_reduce(cmax[:, :], cnt[:, :], AX.X, ALU.max).then_inc(s_cmax, 1)
            flat = "p h c -> p (h c)"
            V.memset(keys[:, 0, :, :], FILL_SRC)
            V.memset(keys[:, 1, :, :], FILL_DST)
            link(V.tensor_tensor(dst_f, dst_f, col_key.rearrange(flat), ALU.add))
            link(V.copy_predicated(keys[:, 1, :, :].rearrange(flat), valid, dst_f))
            link(V.tensor_tensor(dst_f, ends[:, 0, :], col_key.rearrange(flat), ALU.add))
            link(V.copy_predicated(keys[:, 0, :, :].rearrange(flat), valid, dst_f))
            link(V.memset(packed, 0))
            dve.wait_ge(s_call, 1)
            link(V.tensor_scalar(nround[:, 2:3], call[:, :], float(TOP - 1), float(TOP), ALU.add, ALU.max))
            link(V.tensor_scalar(nround[:, 0:1], nround[:, 2:3], 3, None, ALU.arith_shift_right))
            V.tensor_scalar(nround[:, 1:2], nround[:, 0:1], float(RS), None, ALU.max).then_inc(s_nr, 1)
            dve.wait_ge(s_nr, 1)
            rounds = dve.value_load(nround[0:1, 0:1], min_val=1, max_val=ROUNDS_MAX)

            dve.wait_ge(s_par, 16 * NPAR)
            V.memset(one1[:, :], 1.0)
            centre(bqr[:, :], 1, D)
            dve.sem_inc(s_bqp, 1)

            dve.wait_ge(s_sqs, CONT)
            dve.sem_inc(s_bs, 1)
            dve.wait_ge(s_bt, 2)
            V.tensor_scalar(bstat[:, 2, :], psS[0:P, 8:8 + CONT], 1.0 / E, EPS, ALU.mult, ALU.add).then_inc(s_bv, 1)
            dve.wait_ge(s_bv, 2)
            link(V.reciprocal(bstat[:, 3, :], bstat[:, 3, :]))
            link(V.tensor_tensor(bnp[:, 0, :], bnp[:, 0, :], bstat[:, 3, :], ALU.mult))
            for c in range(CONT):
                ins = V.tensor_scalar(cont_f[:, c, :], cont_f[:, c, :], bnp[:, 0, c:c + 1], bnp[:, 1, c:c + 1], ALU.mult, ALU.add)
            link(ins)
            link(V.tensor_copy(cont_part, cont_f))
            dve.sem_inc(s_cxp, 1)

            link(V.tensor_tensor(cont_f, cont_f, cont_part, ALU.subtract))
            dve.wait_ge(s_store, 32)
            link(V.tensor_copy(cont_part, cont_f))
            dve.sem_inc(s_cxp, 1)
            centre(wm[:, 0:D], 128, D)
            centre(wq6[:, :], XROWS, D)
            link(V.tensor_copy(wqp[:, 0, :], wq6[:, :]))
            link(V.tensor_tensor(wq6[:, :], wq6[:, :], wqp[:, 0, :], ALU.subtract))
            link(V.tensor_copy(wqp[:, 1, :], wq6[:, :]))
            link(V.tensor_tensor(wqp[:, 2, :], wq6[:, :], wqp[:, 1, :], ALU.subtract))
            link(V.tensor_scalar(wqr[:, :], wqp[:, 0, :], pmask[:, 0:1], None, ALU.mult))
            link(V.scalar_tensor_tensor(wqr[:, :], wqp[:, 1, :], pmask[:, 1:2], wqr[:, :], ALU.mult, ALU.add))
            link(V.scalar_tensor_tensor(wqx[:, :], wqp[:, 2, :], pmask[:, 2:3], wqr[:, :], ALU.mult, ALU.add))
            V.memset(eps[:, :], EPS)
            link(V.memset(blockones[:, :], 0.0))
            for k in range(2):
                V.memset(blockones[k * D:(k + 1) * D, k * D:(k + 1) * D], 1.0 / D)

            link(V.tensor_tensor(cont_f, cont_f, cont_part, ALU.subtract))
            dve.wait_ge(s_store, 48)
            link(V.tensor_copy(cont_part, cont_f))
            dve.sem_inc(s_cxp, 1)
            link(V.tensor_tensor(gw[:, :], v3[:, 0, :], v3[:, 2, :], ALU.mult))
            link(V.tensor_tensor(wtmp[:, :], wm[:, 0:D], gw[:, :], ALU.mult))
            link(V.tensor_reduce(wm[:, D:D + 1], wtmp[:, :], AX.X, ALU.add))
            link(V.tensor_copy(brow[:, 0:D], v3[0:P, 3, :]))
            centre(brow[:, 0:D], P, D)
            link(V.tensor_tensor(wtmp[0:P, :], brow[:, 0:D], gw[0:P, :], ALU.mult))
            link(V.tensor_reduce(brow[:, D:D + 1], wtmp[0:P, :], AX.X, ALU.add))
            link(V.tensor_tensor(wtmp[0:P, :], v3[0:P, 1, :], v3[0:P, 2, :], ALU.mult))
            link(V.tensor_reduce(k0[:, 0:1], wtmp[0:P, :], AX.X, ALU.add))
            link(V.tensor_tensor(k0[:, 1:2], k0[:, 0:1], bfb[:, :], ALU.add))
            dve.wait_ge(s_bqd, 1)
            V.tensor_copy(bqc[D:2 * D, :], psB[D:2 * D, 0:1])

            dve.wait_ge(s_xo, NCH * -(-(CH // 2) // 4))
            for c in range(2):
                link(V.tensor_copy(xnode[:, :, c * (HI // 2):(c + 1) * (HI // 2)],
                                   psO[c][0:P, 0:HI].rearrange("p (h a) -> p a h", a=2)))
            dve.wait_ge(s_store, 64)
            dve.sem_inc(s_prep, 1)

            PACK_STEPS = 22
            MAGIC = 1.5 * 2 ** 23

            def pack_round(r):
                n = [0]

                def done(ins):
                    n[0] += 1
                    ins.then_inc(s_ext, 1)

                def wait():
                    dve.wait_ge(s_ext, r * PACK_STEPS + (n[0] + PRIME))

                def step(ins):
                    done(ins)
                    wait()

                wait()
                dve.sem_inc(s_own["dve"], 1)
                for a in range(2):
                    for h in range(2):
                        done(V.max(top8[:, a, h, :], keys[:, a, h, :]))
                wait()
                V.tensor_copy(pk[:, :, :], top8[:, :, :, :].rearrange("p a h t -> p a (h t)"))
                for a in range(2):
                    for h in range(2):
                        done(V.match_replace(keys[:, a, h, :], top8[:, a, h, :], keys[:, a, h, :], (FILL_SRC, FILL_DST)[a]))
                wait()
                step(V.tensor_copy(pk_i[:, :, :], pk[:, :, :]))
                step(V.tensor_scalar(pk_c[:, :], pk_i[:, 1, :], 16, None, ALU.arith_shift_right))
                step(V.tensor_scalar(pk_i[:, :, :], pk_i[:, :, :], 0xFFFF, None, ALU.bitwise_and))
                step(V.tensor_copy(rnd[:, 0, :], pk_i[:, 0, :]))
                step(V.tensor_scalar(pk_f[:, 1, :], pk_c[:, :], -256.0, float(2 ** 18), ALU.is_lt, ALU.mult))
                step(V.tensor_tensor(pk_f[:, 0, :], ebase[:, :], pk_c[:, :], ALU.add))
                step(V.tensor_tensor(rnd[:, 2, :], pk_f[:, 0, :], pk_f[:, 1, :], ALU.add))
                pdst, plo, phi = pk_f[:, 0, :], rnd[:, 3, :].bitcast(f32), rnd[:, 4, :].bitcast(f32)
                step(V.tensor_copy(pdst, pk_i[:, 1, :]))
                step(V.tensor_scalar(rnd[:, 1, :], pdst, float(N - 1), None, ALU.min))
                step(V.tensor_scalar(plo, pdst, -(HI - 1) / 2, 1.0 / HI, ALU.add, ALU.mult))
                step(V.tensor_scalar(plo, plo, MAGIC, None, ALU.add))
                step(V.tensor_scalar(plo, plo, MAGIC, None, ALU.subtract))
                step(V.scalar_tensor_tensor(phi, plo, -float(HI), pdst, ALU.mult, ALU.add))
                step(V.tensor_copy(packed[:, :, ds(r * ROUND, ROUND)], rnd[:, :, :]))
                assert n[0] == PACK_STEPS, n[0]

            def graph_half(n, r, h):
                k = passes[n]
                dve.wait_ge(s_hi[k], r * ROUND + (h * TOP + PRIME))
                V.tensor_copy(slotd[h][:, :, :], packed[:, 3:5, ds(r * ROUND + h * TOP, TOP)]).then_inc(s_slotd[k], 1)
                dve.wait_ge(s_slotd[k], 2 * r + (h + 1))
                if n:
                    dve.wait_ge(s_lo[k], r * ROUND + (h * TOP + PRIME))
                V.tensor_tensor(oh_lo8[h][:, :, :],
                                iota16[:, 0:P].rearrange("p (o c) -> p o c", o=1).broadcast_to([P, TOP, P]),
                                slotd[h][:, 0, :].bitcast(f32).rearrange("p (t o) -> p t o", o=1).broadcast_to([P, TOP, P]),
                                ALU.is_equal).then_inc(s_lo8[k], 1)

            def graph_tile(n, r, t):
                k = passes[n]
                h = t // TOP
                if t % TOP == 0:
                    graph_half(n, r, h)
                    if n == 0:
                        dve.wait_ge(s_lo8[k], 2 * r + (h + 1))
                dve.wait_ge(s_ohu[k], r * ROUND + (t + 1))
                V.tensor_scalar(oh_hi[t % GR][:, :], iota16[:, :], slotd[h][:, 1, t % TOP:t % TOP + 1].bitcast(f32), None,
                                ALU.is_equal).then_inc(s_hi[k], 1)

            def node_steps(n):
                both = lambda x: x[:, :].rearrange("p (o h) -> p o h", o=1).broadcast_to([P, 2, HI])
                steps = []
                add = steps.append

                def first():
                    dve.wait_ge(s_pass, n + 1)
                    if n == 0:
                        V.tensor_scalar(degm[:, :], acc[0][0:P, 0:HI], 1.0, None, ALU.max).then_inc(s_degm, 1)
                        V.tensor_scalar(dis[:, :], acc[0][0:P, 0:HI], 0.0, None, ALU.is_gt).then_inc(s_accz, 1)
                    else:
                        for c in range(2):
                            ins = V.scalar_tensor_tensor(xl[:, c, :], acc[c][0:P, 0:HI], us_i[:, 0:1].bitcast(f32), dis[:, :],
                                                         ALU.mult, ALU.mult)
                        ins.then_inc(s_accz, 1)
                    dve.wait_ge(s_accz, n + 1)
                add(first)
                if n == 0:
                    add(lambda: link(V.tensor_scalar(outn[:, :, :], xnode[:, :, :], 1.0 / (LAYERS + 1), None, ALU.mult)))
                    for _ in range(6):
                        add(lambda: None)

                    def inverse():
                        dve.wait_ge(s_degs, 1)
                        link(V.reciprocal(degm[:, :], degm[:, :]))
                    add(inverse)
                    add(lambda: link(V.tensor_tensor(dis[:, :], dis[:, :], degm[:, :], ALU.mult)))
                else:
                    add(lambda: link(V.scalar_tensor_tensor(outn[:, :, :], xl[:, :, :], 1.0 / (LAYERS + 1), outn[:, :, :], ALU.mult, ALU.add)))
                src = xl if n else xnode
                if n < LAYERS:
                    add(lambda: link(V.tensor_tensor(un[:, :, :], src[:, :, :], both(dis), ALU.mult)))
                    add(lambda: V.tensor_reduce(umax[:, 0:1], un[:, :, :], AX.XY, ALU.max, apply_absolute_value=True).then_inc(s_umax, 1))
                    for _ in range(8):
                        add(lambda: None)

                    def scale():
                        dve.wait_ge(s_uall, n + 1)
                        power_scale(us_i, umax[:, 1:2])
                        if n:
                            dve.wait_ge(s_ust, 16 * n)
                    add(scale)
                    s = us_i[:, 1:2].bitcast(f32)
                    table = lambda part: utab[:, :, 2 * part:2 * part + 2].rearrange("p h a -> p a h")
                    add(lambda: link(V.tensor_scalar(part_h[:, :, :], un[:, :, :], s, None, ALU.mult)))
                    add(lambda: link(V.tensor_copy(table(0), part_h[:, :, :])))
                    add(lambda: link(V.scalar_tensor_tensor(part_h[:, :, :], un[:, :, :], s, part_h[:, :, :], ALU.mult, ALU.subtract)))
                    add(lambda: V.tensor_copy(table(1), part_h[:, :, :]).then_inc(s_utab, 1))
                else:
                    def out():
                        dve.wait_ge(s_ust, 16 * LAYERS)
                        V.tensor_copy(otab.rearrange("p h a -> p a h"), outn[:, :, :]).then_inc(s_outt, 1)
                    add(out)
                return steps

            def shift(q, count):
                dve.wait_ge(t_cate[q], count)
                V.tensor_scalar(cate_b[q], cate_b[q], pidx[:, 0:1], None, ALU.subtract).then_inc(t_cm, 1)

            def add_parts(i, q, b):
                dve.wait_ge(t_lo, i * NB + (b + 1))
                V.scalar_tensor_tensor(X[q][b][0:D, :], psA[q][b][0:D, 0:BLK], sc_i[0:D, 0:1].bitcast(f32),
                                       lo_part[b], ALU.mult, ALU.add).then_inc(t_x, 1)

            def free_bank(i, b):
                dve.wait_ge(t_x, i * NB + (b + 1 + PRIME))
                dve.sem_inc(t_Afree, 1)

            def normalise(i, q, b):
                dve.wait_ge(t_sd, i * NB + (b + 1 + PRIME))
                V.tensor_tensor(SD[b], X[q][b][:, :], SD[b], ALU.mult).then_inc(t_xn, 1)

            def last_bias(i, b):
                dve.wait_ge(t_Z, i * NB + (b + 1 + PRIME))
                dve.wait_ge(t_zq, i * NB + PRIME)
                V.tensor_tensor(ZB[b][:, :, :], psZ[0:P, 0:TB * (D + 1)].rearrange("p (t d) -> p t d", t=TB),
                                brow[:, :].rearrange("p (o d) -> p o d", o=1).broadcast_to([P, TB, D + 1]), ALU.add).then_inc(t_zb, 1)

            def last_numerator(i, b):
                dve.wait_ge(t_zb, i * NB + (b + 1 + PRIME))
                V.tensor_copy(num3[:, ds(i * TILES + b * TB, TB)], ZB[b][:, :, D])

            def last_variance(i, b):
                dve.wait_ge(t_zq, i * NB + (b + 1 + PRIME))
                V.tensor_reduce(var3[:, ds(i * TILES + b * TB, TB)], ZQ[b][:, :, :], AX.X, ALU.add).then_inc(t_red, 1)

            def body(i, q, u, cats=(), prev=True, graph=None, nodes=None, last=False):
                if not prev:
                    shift(0, 16)
                if graph and graph[0] == 0:
                    pack_round(graph[1])
                j, p = i - 1, 1 - q
                step = dict(parts=lambda b: add_parts(j, p, b), normalise=lambda b: normalise(j, p, b),
                            bias=lambda b: last_bias(j, b), zvariance=lambda b: last_variance(j, b))
                after = dict(parts=lambda b: free_bank(j, b), bias=lambda b: last_numerator(j, b))
                steps = node_steps(nodes) if nodes is not None else []
                dve.wait_ge(t_cm, i + 1)
                count = NKT - skipped(cats)
                for v, kt, c, jj in one_hot_steps(cats):
                    if kt is not None:
                        dve.wait_ge(t_ohfree, i * NKT + (kt + 1 + (skipped(cats) if kt >= RING else 0)))
                        V.tensor_scalar(onehot[kt % RING], cate_b[q][:, c, :], float(P * jj), None,
                                        ALU.is_equal).then_inc(t_oh, 1 if kt < count - 1 else 1 + skipped(cats))
                    for what, at in AT_DVE.items():
                        if prev and v in at:
                            step[what](at.index(v))
                        if prev and what in after and v - 1 in at:
                            after[what](at.index(v - 1))
                    if graph and v % 3 == 0 and v < 3 * ROUND:
                        graph_tile(graph[0], graph[1], v // 3)
                    if v >= 5 and v - 5 < len(steps):
                        steps[v - 5]()
                    if v == 40 and not last:
                        shift(1 - q, (u + (2 if q else 1)) * 16)

            def between(n):
                with dve.If(rounds > RS):
                    with dve.Fori(RS, rounds) as r:
                        if n == 0:
                            pack_round(r)
                        for t in range(ROUND):
                            graph_tile(n, r, t)

            schedule(dve, body, between)
            i, q = NSB - 1, (NSB - 1) % 2
            for step in (lambda b: add_parts(i, q, b), lambda b: normalise(i, q, b),
                         lambda b: (last_bias(i, b), last_numerator(i, b)), lambda b: last_variance(i, b)):
                for b in range(NB):
                    step(b)
            dve.wait_ge(t_red, NSB * NB + PRIME)
            dve.sem_inc(s_fin, 1)
            dve.wait_ge(s_ydl, 16)
            dve.wait_ge(s_sout, COLS // GSTEP)
            link(V.scalar_tensor_tensor(ys[:, :], yd[:, :], k0[:, 1:2], ys[:, :], ALU.add, ALU.add))
            dve.wait_ge(s_fs, 2)
            link(V.tensor_tensor(num3[:, :], num3[:, :], var3[:, :], ALU.mult))
            V.tensor_tensor(ys[:, :], ys[:, :], num3[:, :], ALU.add).then_inc(s_y, 1)


def kernel(**inputs):
    import numpy as _np
    import concourse.bacc as _bacc
    from concourse import mybir as _mybir
    from concourse.bass_utils import run_bass_kernel_spmd as _run

    a = {k.replace("L0_rec_", ""): _np.ascontiguousarray(v) for k, v in inputs.items()}
    edges = a["r_edge_index"]
    by_superblock = lambda x: _np.ascontiguousarray(
        x.reshape(x.shape[0], P, NSB, TILES).transpose(2, 0, 3, 1).reshape(NSB, -1))
    arrays = {
        "src": edges[0].reshape(P, COLS), "dst": edges[1].reshape(P, COLS),
        "cate": by_superblock(a["r_cate_features"]),
        "cate_tiles": _np.ascontiguousarray(
            a["r_cate_features"].reshape(CATE, P, NSB, TILES).transpose(2, 1, 0, 3).reshape(NSB, P, CATE * TILES)),
        "cont": by_superblock(a["cont_features"]),
        "node": a["node_emb"].reshape(P, HI * D), "tabT": _np.ascontiguousarray(a["cate_table"].T),
        "Wc": _np.ascontiguousarray(a["Wc"].reshape(CATE, D, D).transpose(1, 0, 2).reshape(D, CATE * D)),
        "bc": a["bc"], "ln1_g": a["ln1_g"], "ln1_b": a["ln1_b"], "bn_g": a["bn_g"], "bn_b": a["bn_b"],
        "Wq6": _np.ascontiguousarray(_np.broadcast_to(a["Wq"], (len(XPARTS), CONT, D)).reshape(XROWS, D)),
        "mask": _np.repeat(_np.eye(3, dtype=_np.float32)[[w for _, w in XPARTS]], CONT, axis=0),
        "bq": a["bq"], "ln2_g": a["ln2_g"], "ln2_b": a["ln2_b"], "Wm": a["Wm"], "bm": a["bm"],
        "ln3_g": a["ln3_g"], "ln3_b": a["ln3_b"], "Wf": a["Wf"].reshape(3 * D), "bf": a["bf"],
    }
    nc = _bacc.Bacc("TRN2", target_bir_lowering=False, num_devices=1)
    args = []
    for name, x in arrays.items():
        args.append(nc.dram_tensor(f"in_{name}", x.shape, _mybir.dt.from_np(x.dtype), kind="ExternalInput").ap())
    args.append(nc.dram_tensor("out_y", (P, COLS), _mybir.dt.float32, kind="ExternalOutput").ap())
    rec_kernel(nc, *args)
    r = _run(nc, [{f"in_{k}": v for k, v in arrays.items()}], core_ids=[0])
    return r.results[0]["out_y"].reshape(E)
```

```python
import concourse.bass as bass
from concourse import mybir
from contextlib import ExitStack
import numpy as np

N = 62500
D = 64
E = 125000
OFF = 1250
CATE = 5
CONT = 8
LAYERS = 3
EPS = 1e-5
P = 125
COLS = E // P
HI = N // P
HALF = COLS // 2
TOP = 8
ROUND = 2 * TOP
ROUNDS_MAX = -(-HALF // TOP)
RS_DEG = 11
RS = 10
LISTW = (ROUNDS_MAX + 1) * ROUND
FILL_SRC = -float(2 ** 25)
FILL_DST = -float(2 ** 25) + 65534.0
SB = 1000
TILES = SB // P
NSB = E // SB
BLK = 500
NB = SB // BLK
KT = OFF // P
NKT = CATE * KT
RING = 10
GR = 4
GRH = 8
TB = BLK // P
PRIME = 1
LOADED = (2, 3, 4)
CATS = (4, 3, 2)
GATHERED = dict(deg=((0, 1, 2), (0, 1, 2)), layer=((0, 1), (0,)), nodes=((0, 1, 2),), tail=((0, 1), (0, 1)))
TAIL_PAIRS = 9
GSTEP = 10
XROWS = 6 * CONT
XPARTS = ((0, 0), (0, 1), (0, 2), (1, 0), (1, 1), (2, 0))
AT_PE = dict(variance=(8, 13), feature=(19, 26), product=(21, 28))
AT_ACT = dict(lo=(0, 1), square=(3, 4), rstd=(9, 14), relu=(12, 17), feature=(20, 27), zsquare=(24, 31))
AT_DVE = dict(parts=(10, 12), normalise=(21, 26), bias=(32, 39), zvariance=(41, 46))
AT_CATS = (24, 40, 46)
AT_NODES = (10, 18, 26, 34, 42)
AT_NODES_LOAD = (0, 1, 12, 20, 28)
AT_NODES_COPY = 47
NPAIR = 5
AT_TILE = [5 + 44 * t // (ROUND - 1) for t in range(ROUND)]
ACT_LEAD = 8
F_MAX = 13


def rec_kernel(nc, src_e, dst_e, cate, cate_tiles, cont, node_emb, tableT, Wc, bc, ln1_g, ln1_b, bn_g, bn_b,
               Wq6, partmask, bq, ln2_g, ln2_b, Wm, bm, ln3_g, ln3_b, Wf, bf, y):
    f32, bf16, f16, i32 = mybir.dt.float32, mybir.dt.bfloat16, mybir.dt.float16, mybir.dt.int32
    ALU, ACT, AX = mybir.AluOpType, mybir.ActivationFunctionType, mybir.AxisListType
    RMAX = bass.bass_isa.ReduceOp.max
    ds = bass.ds
    ctx = ExitStack()
    with ctx:
        def sb(name, shape, dt=f32):
            return ctx.enter_context(nc.sbuf_tensor(name, shape, dt))

        def sem(name):
            return ctx.enter_context(nc.semaphore(name))

        cate16_d = nc.dram_tensor("cate16_d", [NSB, CATE * SB], f16, kind="Internal").ap()
        T16_d = [nc.dram_tensor(f"T16_{c}_d", [OFF, 2 * D], f16, kind="Internal").ap() for c in CATS]
        cxp_d = [nc.dram_tensor(f"cxp{k}_d", [NSB, CONT * SB], bf16, kind="Internal").ap() for k in range(3)]
        u_d = [nc.dram_tensor(f"u{l}_d", [N, 4], f32, kind="Internal").ap() for l in range(LAYERS)]
        out_d = nc.dram_tensor("out_d", [N, 2], f32, kind="Internal").ap()
        yd_d = nc.dram_tensor("yd_d", [E, 1], f32, kind="Internal").ap()

        def views(area):
            at = [0]

            def take(shape, dt=f32):
                words = int(np.prod(shape[1:])) * (2 if dt in (f16, bf16) else 4) // 4
                v = area[0:shape[0], at[0]:at[0] + words]
                at[0] += words
                assert at[0] <= area.shape[1], (at[0], area.shape)
                if dt != f32:
                    v = v.bitcast(dt)
                if len(shape) > 2:
                    names = "abcd"[:len(shape) - 1]
                    v = v.rearrange(f"p ({' '.join(names)}) -> p {' '.join(names)}", **dict(zip(names, shape[1:])))
                return v
            return take

        wide = sb("wide", [128, 15500])
        take = views(wide)
        cont_f = take([P, CONT, SB])
        cate_i = take([P, CATE * SB], i32)
        cate_h = take([P, CATE * SB], f16)
        take = views(wide)
        take([P, CONT * SB])
        cont_part = take([P, CONT, SB], bf16)
        take = views(wide)
        onehot = [take([P, SB], f16) for _ in range(RING)]
        lo_part = [take([D, BLK]) for _ in range(NB)]
        SD = [take([128, BLK]) for _ in range(NB)]
        R = [take([128, BLK]) for _ in range(NB)]
        cx = [take([XROWS, SB], bf16) for _ in range(2)]
        cate_b = [None, take([P, CATE, SB], f16)]
        rowsT = [take([P, TILES, 2 * D], f16) for _ in CATS[:2]]
        take = views(wide[:, CONT * SB + CATE * SB:])
        cate_b[0] = take([P, CATE, SB], f16)
        listmem = sb("listmem", [P, 5 * LISTW])
        take = views(listmem)
        tabT = take([D, OFF])
        Tf = take([P, KT, CATE, D])
        take = views(listmem)
        col_key = take([P, 2, HALF])
        valid = take([P, COLS], i32)
        dst_f = take([P, COLS])
        packed = views(listmem)([P, 5, LISTW], i32)
        nodemem = sb("nodemem", [128, 4 * HI + TILES * D])
        take = views(nodemem)
        nchunk = [take([128, NPAIR, P]) for _ in range(2)]
        take = views(nodemem)
        utab = take([P, HI, 4])
        rowsT.append(take([P, TILES, 2 * D], f16))
        otab = views(nodemem)([P, HI, 2])

        ends = sb("ends", [P, 2, COLS], i32)
        keys = sb("keys", [P, 2, 2, HALF])
        top8 = sb("top8", [P, 2, 2, TOP])
        pk = sb("pk", [P, 2, ROUND])
        pk_i = sb("pk_i", [P, 2, ROUND], i32)
        pk_c = sb("pk_c", [P, ROUND], i32)
        pk_f = sb("pk_f", [P, 2, ROUND])
        rnd = sb("rnd", [P, 5, ROUND], i32)
        ebase = sb("ebase", [P, ROUND])
        ebase_i = sb("ebase_i", [P, ROUND], i32)
        cnt = sb("cnt", [P, 2])
        cmax = sb("cmax", [P, 2])
        cleft = sb("cleft", [P, 2])
        flag = sb("flag", [P, 1])
        merged = sb("merged", [P, 5, ROUND], i32)
        isfirst = sb("isfirst", [P, ROUND], i32)
        mergeable = sb("mergeable", [P, ROUND], i32)
        call = sb("call", [P, 2])
        nround = sb("nround", [P, 3], i32)
        slot = [sb(f"slot{h}", [P, TOP], i32) for h in range(2)]
        slotd = [sb(f"slotd{h}", [P, 2, TOP], i32) for h in range(2)]
        gath = [sb(f"gath{h}", [P, TOP, 4]) for h in range(2)]
        oh_hi = [sb(f"oh_hi{k}", [P, HI], f16) for k in range(GRH)]
        oh_lo8 = [sb(f"oh_lo8{h}", [P, TOP, P], f16) for h in range(2)]
        oh_lo = [sb(f"oh_lo{k}", [P, 4, P], f16) for k in range(GR)]
        iota_i = sb("iota_i", [P, 2, HALF], i32)
        iota16 = sb("iota16", [P, HI], f16)
        zero_l = sb("zero_l", [P, P], f16)
        slot_c = [sb(f"slot_cate{q}", [P, len(CATS), TILES], i32) for q in range(2)]
        ident16 = sb("ident16", [P, P], f16)
        ident = sb("ident", [P, P])
        w4 = sb("w4", [128, 4])
        xnode = sb("xnode", [P, 2, HI])
        outn = sb("outn", [P, 2, HI])
        dis = sb("dis", [P, HI])
        degm = sb("degm", [P, HI])
        un = sb("un", [P, 2, HI])
        xl = sb("xl", [P, 2, HI])
        part_h = sb("part_h", [P, 2, HI], f16)
        umax = sb("umax", [P, 2])
        us_i = sb("us_i", [P, 2], i32)
        slot_d2 = [sb(f"slot_dst{h}", [P, 2, TOP], i32) for h in range(2)]
        gd = [sb(f"gd{h}", [P, TOP, 2]) for h in range(2)]
        slot_s = [sb(f"slot_src{q}", [P, GSTEP], i32) for q in range(2)]
        gs = [sb(f"gs{q}", [P, GSTEP, 2]) for q in range(2)]
        dlast = sb("dlast", [P, 1])
        ys = sb("ys", [P, COLS])
        yd = sb("yd", [P, COLS])

        bstat = sb("bstat", [P, 4, CONT])
        sqj = sb("sqj", [P, SB])
        bnp = sb("bnp", [P, 2, CONT])
        onesm = sb("onesm", [P, P])
        pidx_i = sb("pidx_i", [P, 1], i32)
        pidx = sb("pidx", [P, 1])
        wc = sb("wc", [D, CATE, D])
        wsum = sb("wsum", [128, 8])
        T16 = sb("T16", [P, KT, CATE, 2 * D], f16)
        bcb = sb("bcb", [P, D])
        tmax = sb("tmax", [128, 2])
        sc_i = sb("sc_i", [128, 2], i32)
        wq6 = sb("wq6", [XROWS, D])
        wqp = sb("wqp", [XROWS, 3, D], bf16)
        wqx = sb("wqx", [XROWS, D], bf16)
        wqr = sb("wqr", [XROWS, D])
        pmask = sb("pmask", [XROWS, 3])
        bqr = sb("bqr", [1, D])
        one1 = sb("one1", [1, 1])
        bqc = sb("bqc", [128, 1])
        g12 = sb("g12", [128, 1])
        b12 = sb("b12", [128, 1])
        eps = sb("eps", [128, 1])
        wm = sb("wm", [128, D + 1])
        gw = sb("gw", [128, D])
        wtmp = sb("wtmp", [128, D])
        brow = sb("brow", [P, D + 1])
        v3 = sb("v3", [128, 4, D])
        bfb = sb("bfb", [P, 1])
        k0 = sb("k0", [P, 2])
        blockones = sb("blockones", [128, 128])
        X = [[sb(f"X{q}{b}", [128, BLK]) for b in range(NB)] for q in range(2)]
        SQ = [sb(f"SQ{b}", [128, BLK]) for b in range(NB)]
        ZB = [sb(f"ZB{b}", [P, TB, D + 1]) for b in range(NB)]
        ZQ = [sb(f"ZQ{b}", [P, TB, D]) for b in range(NB)]
        var3 = sb("var3", [P, COLS])
        num3 = sb("num3", [P, COLS])

        bank = [ctx.enter_context(nc.psum_tensor(f"bank{k}", [128, 512], f32)) for k in range(8)]
        psA = [[bank[2 * q + b] for b in range(NB)] for q in range(2)]
        acc = [bank[4], bank[5]]
        psCV, psZ = bank[6], bank[7]
        psT, psS, psB = [bank[0], bank[1]], bank[6], bank[7]
        psO = bank[5]

        s_ends, s_cate, s_cont, s_par, s_tabT = sem("ends_loaded"), sem("cate_loaded"), sem("cont_loaded"), sem("params_loaded"), sem("tabT_loaded")
        s_w4, s_first = sem("w4_loaded"), sem("wc_bc_loaded")
        s_nch = [sem(f"nodes_loaded{k}") for k in range(2)]
        s_iota, s_dve, s_id = sem("iotas_ready"), sem("dve_chain"), sem("ident_ready")
        s_nfree, s_xev = [sem(f"nodes_projected{k}") for k in range(2)], sem("projection_copied")
        s_cmax, s_call, s_nr = sem("counts_ready"), sem("counts_reduced"), sem("rounds_ready")
        s_keyfill = sem("keys_filled")
        s_cateh, s_cxp, s_store = sem("cate16_ready"), sem("features_part_ready"), sem("scratch_stored")
        s_bs, s_bt, s_bsq, s_sqs, s_bv = sem("bn_sums"), sem("bn_totals"), sem("bn_centred"), sem("bn_squares"), sem("bn_sqrt")
        s_wc, s_tps, s_tev = sem("wc_ready"), sem("T_product"), sem("T_copied")
        s_tmax, s_tall, s_bqp, s_bqd = sem("tmax_ready"), sem("tmax_reduced"), sem("bq_ready"), sem("bq_column")
        s_prep, s_ready = sem("setup_done"), sem("graph_constants_ready")
        passes = ["deg"] + [f"l{l}" for l in range(LAYERS)]
        s_slotd = {k: sem(f"slotd_ready_{k}") for k in passes}
        s_slotp = [sem(f"slot_ready{l}") for l in range(LAYERS)]
        s_gath = {k: [sem(f"gathered_{k}{h}") for h in range(2)] for k in passes[1:]}
        s_lo8 = {k: sem(f"lo8_ready_{k}") for k in passes}
        s_hi = {k: sem(f"hi_ready_{k}") for k in passes}
        s_lo = {k: sem(f"lo_ready_{k}") for k in passes[1:]}
        s_ohu = {k: sem(f"onehots_used_{k}") for k in passes}
        s_ext = sem("pack_chain")
        s_pass, s_accz = sem("pass_done"), sem("acc_read")
        s_degm, s_degs = sem("deg_ready"), sem("deg_sqrt")
        s_umax, s_uall, s_utab, s_ust = sem("umax_ready"), sem("umax_reduced"), sem("utab_ready"), sem("utab_stored")
        s_outt, s_outst, s_dl, s_ydf, s_ydst = sem("out_ready"), sem("out_stored"), sem("dlast_loaded"), sem("yd_filled"), sem("yd_stored")
        s_dslot, s_dsc, s_ydl = sem("dst_slots_ready"), [sem("d_scattered0"), sem("d_scattered1")], sem("yd_loaded")
        s_dg = [sem("d_gathered0"), sem("d_gathered1")]
        s_sslot, s_sg, s_sout = sem("src_slots_ready"), [sem("s_gathered0"), sem("s_gathered1")], sem("ys_copied")
        s_own = {e: sem(f"carries_waits_{e}") for e in ("dve", "pool", "sp", "pe", "act")}
        t_cate = [sem(f"t_cate_loaded{q}") for q in range(2)]
        t_cx = [sem(f"t_cx_loaded{q}") for q in range(2)]
        t_ci = [sem(f"t_cate_tiles_loaded{q}") for q in range(2)]
        t_rows = [sem(f"t_T_rows_gathered{g}") for g in range(len(CATS))]
        t_rowsfree = [sem(f"t_T_rows_used{g}") for g in range(len(CATS))]
        s_t16, s_t16st = sem("T16_ready"), sem("T16_stored")
        t_cm = sem("t_cate_shifted")
        t_oh, t_ohfree = sem("t_onehot_ready"), sem("t_onehot_free")
        t_A, t_Afree = sem("t_A_done"), sem("t_A_evacuated")
        t_C, t_Cfree = sem("t_C_done"), sem("t_C_evacuated")
        t_lo, t_x = sem("t_lo_copied"), sem("t_x_ready")
        t_sq, t_V, t_ln, t_sd = sem("t_square_ready"), sem("t_V_done"), sem("t_ln_ready"), sem("t_sd_ready")
        t_xn, t_R = sem("t_xn_ready"), sem("t_R_ready")
        t_Z, t_zb, t_zq, t_red = sem("t_Z_done"), sem("t_zb_ready"), sem("t_zq_ready"), sem("t_zq_reduced")
        s_fin, s_fs, s_y, s_out = sem("fin_var"), sem("fin_rstd"), sem("y_ready"), sem("y_stored")
        primed = [*t_rowsfree, *s_nfree, s_xev, t_x, t_V, t_ln, t_sd, t_xn, t_Z, t_zb, t_zq, t_red, t_Cfree, t_R, s_ext]
        BACK = TOP + PRIME

        block = ctx.enter_context(nc.Block())

        def rows(v, n, parts):
            return v.rearrange("(o c) -> o c", o=1).broadcast_to([parts, n])

        NPAR = 15
        NODE_SB = len(GATHERED["nodes"])
        RSN = [RS_DEG] + [RS] * LAYERS
        TAIL = 1 + sum(RSN) + len(passes) * NODE_SB

        def schedule(eng, body, between, middle=None):
            used = [0] * len(CATS)

            def pair(it, i, sets, what=({}, {})):
                per = [sum(g in s for s in sets) for g in range(len(CATS))]
                for k in range(2):
                    cats = [(g, it * per[g] + (used[g] + (k if g in sets[0] else 0))) for g in sets[k]]
                    body(2 * it + (i + k), (i + k) % 2, it + (i + k) // 2, cats=cats, **what[k])
                return per

            def pairs(n, i, sets, what=lambda it: ({}, {})):
                with eng.Fori(0, n) as it:
                    per = pair(it, i, sets, what(it))
                for g in range(len(CATS)):
                    used[g] += n * per[g]

            def single(i, sets, what):
                body(i, i % 2, i // 2, cats=[(g, used[g]) for g in sets], **what)
                for g in sets:
                    used[g] += 1

            body(0, 0, 0, prev=False)
            for n in range(len(passes)):
                more = lambda it, k: dict(project=(it, k)) if n == 0 else {}
                i0 = 1 + sum(RSN[:n]) + n * NODE_SB
                sets = GATHERED["layer" if n else "deg"]
                pairs(RSN[n] // 2, i0, sets, lambda it: [dict(graph=(n, 2 * it + k), **more(it, k)) for k in range(2)])
                for r in range(RSN[n] // 2 * 2, RSN[n]):
                    single(i0 + r, sets[0], dict(graph=(n, r)))
                between(n)
                for k in range(NODE_SB):
                    single(i0 + RSN[n] + k, GATHERED["nodes"][k], {} if k else dict(nodes=n))
            odd = (NSB - TAIL) % 2
            if odd:
                single(TAIL, (), {})
            if middle:
                middle()
            else:
                pairs((NSB - TAIL) // 2 - TAIL_PAIRS, TAIL + odd, ((), ()))
            if TAIL_PAIRS > 1:
                pairs(TAIL_PAIRS - 1, NSB - 2 * TAIL_PAIRS, GATHERED["tail"])
            pair(0, NSB - 2, GATHERED["tail"], ({}, dict(last=True)))

        def one_hot_steps(cats):
            left = [c for c in range(CATE) if c not in [CATS[g] for g, _ in cats]]
            n = len(left) * KT
            for v in range(NKT):
                kt = v * n // NKT
                new = v == 0 or kt != (v - 1) * n // NKT
                yield (v, kt if new else None, left[kt // KT], kt % KT)

        assert RS_DEG // 2 * 2 * len(AT_NODES) * NPAIR * 2 == HI

        def node_step(project, s):
            it, k = project
            m = len(AT_NODES) * k + s
            return m % 2, it * len(AT_NODES) + m // 2

        def skipped(cats):
            return len(cats) * KT

        @block.sync
        def _(sp):
            sp.dma_start(wc[:, :, :], Wc.rearrange("d (c k) -> d c k", c=CATE)).then_inc(s_first, 16)
            sp.dma_start(bcb[:, :], rows(bc, D, P)).then_inc(s_first, 16)
            sp.dma_start(tabT, tableT).then_inc(s_tabT, 16)
            sp.dma_start(cate_i, cate).then_inc(s_cate, 16)
            sp.dma_start(cont_f, cont.rearrange("s (c k) -> s c k", c=CONT)).then_inc(s_cont, 16)

            def par(dst, src):
                sp.dma_start(dst, src).then_inc(s_par, 16)

            par(bnp[:, 0, :], rows(bn_g, CONT, P))
            par(bnp[:, 1, :], rows(bn_b, CONT, P))
            par(wq6[:, :], Wq6)
            par(pmask[:, :], partmask)
            par(bqr[:, :], rows(bq, D, 1))
            for k, (g, b) in enumerate(((ln1_g, ln1_b), (ln2_g, ln2_b))):
                par(g12[D * k:D * k + D, :], g.rearrange("(c o) -> c o", o=1))
                par(b12[D * k:D * k + D, :], b.rearrange("(c o) -> c o", o=1))
            par(wm[:, 0:D], Wm)
            for k, v in enumerate((ln3_g, ln3_b, Wf[2 * D:3 * D], bm)):
                par(v3[:, k, :], rows(v, D, 128))
            par(bfb[:, :], rows(bf, 1, P))
            sp.wait_ge(s_cateh, 1)
            sp.dma_start(cate16_d, cate_h).then_inc(s_store, 16)
            sp.wait_ge(s_t16, 1)
            for k, c in enumerate(CATS):
                sp.dma_start(T16_d[k].rearrange("(j p) k -> p j k", p=P), T16[:, :, c, :]).then_inc(s_t16st, 16)
            def load(i, q):
                load_cate(i, q)
                load_features(i, q)

            def load_cate(i, q):
                sp.dma_start(cate_b[q],
                             cate16_d[ds(i, 1), :].broadcast_to([P, CATE * SB]).rearrange("p (c k) -> p c k", c=CATE)).then_inc(t_cate[q], 16)

            def load_features(i, q):
                for g, (a, _) in enumerate(XPARTS):
                    sp.dma_start(cx[q][g * CONT:(g + 1) * CONT, :],
                                 cxp_d[a][ds(i, 1), :].rearrange("o (c k) -> (o c) k", c=CONT)).then_inc(t_cx[q], 16)

            sp.wait_ge(s_store, 16)
            load_cate(0, 0)
            for k in range(3):
                sp.wait_ge(s_cxp, k + 1)
                sp.dma_start(cxp_d[k].rearrange("s (c k) -> s c k", c=CONT), cont_part).then_inc(s_store, 16)

            def load_tiles(i, q):
                sp.dma_start(slot_c[q][:, :, :], cate_tiles[ds(i, 1), :, :].rearrange("o p (c t) -> (o p) c t", c=CATE)[:, CATE - len(CATS):CATE, :]).then_inc(t_ci[q], 16)

            sp.wait_ge(s_prep, 1)
            sp.wait_ge(s_store, 64)
            load_features(0, 0)
            load(1, 1)
            load_tiles(1, 1)

            def body(i, q, u, cats=(), prev=True, graph=None, project=None, nodes=None, last=False):
                if not prev or last:
                    return
                sp.wait_ge(t_oh, i * NKT)
                sp.sem_inc(s_own["sp"], 1)
                sp.wait_ge(t_C, i * NB)
                sp.sem_inc(s_own["sp"], 1)
                load(i + 1, 1 - q)
                sp.wait_ge(t_ohfree, i * NKT + RING)
                sp.sem_inc(s_own["sp"], 1)
                load_tiles(i + 1, 1 - q)

            schedule(sp, body, lambda n: None)
            sp.wait_ge(s_y, 1)
            sp.dma_start(y, ys[:, :]).then_inc(s_out, 16)
            sp.wait_ge(s_out, 16)

        @block.gpsimd
        def _(pool):
            G = nc.gpsimd
            G.iota(pidx_i[:, :], pattern=[[0, 1]], base=0, channel_multiplier=1).then_inc(s_iota, 1)
            G.iota(iota_i[:, :, :], pattern=[[0, 2], [1, HALF]], base=0, channel_multiplier=0).then_inc(s_iota, 1)
            G.iota(ebase_i[:, :], pattern=[[HALF, 2], [0, TOP]], base=256, channel_multiplier=COLS).then_inc(s_iota, 1)
            G.memset(ident[:, :], 0.0).then_inc(s_id, 1)
            pool.wait_ge(s_id, 1)
            G.affine_select(out=ident[:, :], in_=ident[:, :], compare_op=ALU.not_equal, fill=1.0, base=0,
                            pattern=[[-1, P]], channel_multiplier=1).then_inc(s_id, 1)
            G.memset(keys[:, 0, :, :], FILL_SRC)
            G.memset(keys[:, 1, :, :], FILL_DST).then_inc(s_keyfill, 1)
            pool.wait_ge(s_cate, 16)
            G.tensor_copy(cate_h, cate_i).then_inc(s_cateh, 1)
            pool.wait_ge(s_tmax, 1)
            G.partition_all_reduce(tmax[:, 1:2], tmax[:, 0:1], 128, RMAX).then_inc(s_tall, 1)
            pool.wait_ge(s_cmax, 1)
            G.partition_all_reduce(call[:, :], cmax[:, :], P, RMAX).then_inc(s_call, 1)
            pool.wait_ge(s_nr, 1)
            rounds = pool.value_load(nround[0:1, 1:2], min_val=RS, max_val=ROUNDS_MAX)

            def gather(out, table, index, done):
                G.indirect_dma_start(out=out, out_offset=None, in_=table,
                                     in_offset=bass.IndirectOffsetOnAxis(index, 0)).then_inc(done, 16)

            def table(l, meanwhile):
                pool.wait_ge(s_umax, l + 1)
                G.partition_all_reduce(umax[:, 1:2], umax[:, 0:1], P, RMAX).then_inc(s_uall, 1)
                for rows in meanwhile:
                    rows()
                pool.wait_ge(s_utab, l + 1)
                pool.dma_start(u_d[l].rearrange("(p h) k -> p h k", p=P), utab).then_inc(s_ust, 16)
                pool.wait_ge(s_ust, 16 * (l + 1))

            def graph_half(n, r, h):
                k = passes[n]
                pool.wait_ge(s_lo[k], r * ROUND + (h * TOP + PRIME))
                pool.sem_inc(s_own["pool"], 1)
                G.tensor_copy(slot[h][:, :], packed[:, 0, ds(r * ROUND + h * TOP, TOP)]).then_inc(s_slotp[n - 1], 1)
                pool.wait_ge(s_slotp[n - 1], 2 * r + (h + 1))
                pool.sem_inc(s_own["pool"], 1)
                for t in range(TOP):
                    gather(gath[h][:, t, :], u_d[n - 1], slot[h][:, t:t + 1], s_gath[k][h])

            def rows_of(g, used, q, u):
                pool.wait_ge(t_ci[q], (u + (1 if q else 0)) * 16)
                pool.wait_ge(t_rowsfree[g], used + PRIME)
                pool.sem_inc(s_own["pool"], 1)
                for t in range(TILES):
                    gather(rowsT[g][:, t, :], T16_d[g], slot_c[q][:, LOADED.index(CATS[g]), t:t + 1], t_rows[g])

            def body(i, q, u, cats=(), prev=True, graph=None, project=None, nodes=None, last=False):
                ways = [lambda g=g, used=used: rows_of(g, used, q, u) for g, used in cats]
                if graph and graph[0]:
                    graph_half(graph[0], graph[1], 0)
                for rows in ways[:1]:
                    rows()
                if graph and graph[0]:
                    graph_half(graph[0], graph[1], 1)
                for rows in ways[1:2]:
                    rows()
                if nodes is not None and nodes < LAYERS:
                    table(nodes, ways[2:])
                else:
                    for rows in ways[2:]:
                        rows()

            def between(n):
                if n:
                    with pool.If(rounds > RS):
                        with pool.Fori(RS, rounds) as r:
                            for h in range(2):
                                graph_half(n, r, h)

            def out_gathers():
                pool.wait_ge(s_outt, 1)
                pool.dma_start(out_d.rearrange("(p h) k -> p h k", p=P), otab).then_inc(s_outst, 16)
                pool.wait_ge(s_outst, 16)
                pool.dma_start(dlast[:, :], out_d[N - 1:N, 1:2].broadcast_to([P, 1])).then_inc(s_dl, 16)
                G.memset(yd[:, :], 0.0).then_inc(s_ydf, 1)
                pool.wait_ge(s_dl, 16)
                pool.wait_ge(s_ydf, 1)
                G.tensor_scalar(yd[:, :], yd[:, :], dlast[:, 0:1], None, ALU.add).then_inc(s_ydf, 1)
                pool.wait_ge(s_ydf, 2)
                pool.dma_start(yd_d.rearrange("(p c) o -> p (c o)", p=P), yd[:, :]).then_inc(s_ydst, 16)
                pool.wait_ge(s_ydst, 16)
                def dst_round(r, first):
                    for h in range(2):
                        if not first:
                            pool.wait_ge(s_dsc[h], r * (16 * TOP))
                            pool.sem_inc(s_own["pool"], 1)
                        G.tensor_copy(slot_d2[h][:, :, :], packed[:, 1:3, ds(r * ROUND + h * TOP, TOP)]).then_inc(s_dslot, 1)
                        pool.wait_ge(s_dslot, 2 * r + (h + 1))
                        pool.sem_inc(s_own["pool"], 1)
                        for t in range(TOP):
                            gather(gd[h][:, t, :], out_d, slot_d2[h][:, 0, t:t + 1], s_dg[h])
                    for h in range(2):
                        pool.wait_ge(s_dg[h], r * (16 * TOP) + 16 * TOP)
                        pool.sem_inc(s_own["pool"], 1)
                        for t in range(TOP):
                            G.indirect_dma_start(out=yd_d, out_offset=bass.IndirectOffsetOnAxis(slot_d2[h][:, 1, t:t + 1], 0),
                                                 in_=gd[h][:, t, 1:2], in_offset=None,
                                                 bounds_check=E - 1, oob_is_err=False).then_inc(s_dsc[h], 16)

                dst_round(0, True)
                with pool.Fori(1, rounds) as r:
                    dst_round(r, False)
                for h in range(2):
                    pool.wait_ge(s_dsc[h], rounds * (16 * TOP))
                    pool.sem_inc(s_own["pool"], 1)
                pool.dma_start(yd[:, :], yd_d.rearrange("(p c) o -> p (c o)", p=P)).then_inc(s_ydl, 16)

                def src_step(c, q, first):
                    if not first:
                        src_out(c, q)
                    G.tensor_copy(slot_s[q][:, :], ends[:, 0, ds(c * GSTEP, GSTEP)]).then_inc(s_sslot, 1)
                    pool.wait_ge(s_sslot, c + 1)
                    pool.sem_inc(s_own["pool"], 1)
                    for t in range(GSTEP):
                        gather(gs[q][:, t, :], out_d, slot_s[q][:, t:t + 1], s_sg[q])

                def src_out(c, q):
                    pool.wait_ge(s_sg[q], (c - q) * (8 * GSTEP))
                    pool.sem_inc(s_own["pool"], 1)
                    G.tensor_copy(ys[:, ds((c - 2) * GSTEP, GSTEP)], gs[q][:, :, 0]).then_inc(s_sout, 1)
                    pool.wait_ge(s_sout, c - 1)
                    pool.sem_inc(s_own["pool"], 1)

                NSTEP = COLS // GSTEP
                src_step(0, 0, True)
                src_step(1, 1, True)
                with pool.Fori(1, NSTEP // 2) as it:
                    src_step(2 * it, 0, False)
                    src_step(2 * it + 1, 1, False)
                src_out(NSTEP, 0)
                src_out(NSTEP + 1, 1)

            pool.wait_ge(s_t16st, 16 * len(CATS))
            schedule(pool, body, between, middle=out_gathers)

        @block.tensor
        def _(pe):
            mm = nc.tensor.matmul
            pe.wait_ge(s_wc, 1)
            pe.wait_ge(s_tabT, 16)
            for j in range(KT):
                if j >= 2:
                    pe.wait_ge(s_tev, j - 1)
                mm(psT[j % 2][0:P, 0:CATE * D], lhsT=tabT[:, j * P:(j + 1) * P], rhs=wc[:, :, :].rearrange("d c k -> d (c k)"),
                   start=True, stop=True).then_inc(s_tps, 1)

            def bn_total(k):
                pe.wait_ge(s_bs, k + 1)
                mm(psS[0:P, 8 * k:8 * k + CONT], lhsT=onesm[:, :], rhs=bstat[:, k, :], start=True, stop=True).then_inc(s_bt, 1)

            bn_total(0)
            pe.wait_ge(s_bqp, 1)
            mm(psB[D:2 * D, 0:1], lhsT=bqr[:, :], rhs=one1[:, :], start=True, stop=True).then_inc(s_bqd, 1)
            bn_total(1)
            pe.wait_ge(s_w4, 65)

            pe.wait_ge(s_ready, 1)
            pe.wait_ge(s_nr, 1)
            deg_rounds = pe.value_load(nround[0:1, 0:1], min_val=1, max_val=ROUNDS_MAX)
            rounds = pe.value_load(nround[0:1, 1:2], min_val=RS, max_val=ROUNDS_MAX)
            pe.wait_ge(s_prep, 1)

            def zero_product(c, start):
                return mm(acc[c][0:P, 0:HI], lhsT=zero_l[:, :], rhs=iota16[:, :], start=start, stop=not start,
                          skip_group_check=True)

            def pass_start(n):
                if n:
                    pe.wait_ge(s_accz, n)
                    pe.wait_ge(s_xev, RS_DEG // 2 * 2 + PRIME)
                for c in range(2 if n else 1):
                    zero_product(c, True)

            def graph_tile(n, r, t):
                k = passes[n]
                pe.wait_ge(s_hi[k], r * ROUND + (t + 1 + PRIME))
                if n:
                    pe.wait_ge(s_lo[k], r * ROUND + (t + 1 + BACK))
                    for v in range(4):
                        last = mm(acc[v % 2][0:P, 0:HI], lhsT=oh_lo[t % GR][:, v, :], rhs=oh_hi[t % GRH][:, :],
                                  start=False, stop=False, skip_group_check=True)
                else:
                    last = mm(acc[0][0:P, 0:HI], lhsT=oh_lo8[t // TOP][:, t % TOP, :], rhs=oh_hi[t % GRH][:, :],
                              start=False, stop=False, skip_group_check=True)
                last.then_inc(s_ohu[k], 1)

            def project_nodes(project, r, s):
                buf, used = node_step(project, s)
                if s == 0:
                    pe.wait_ge(s_xev, r + PRIME)
                pe.wait_ge(s_nch[buf], used * 16 + 16)
                for t in range(NPAIR):
                    at = 4 * (s * NPAIR + t)
                    last = mm(psO[0:P, at:at + 4], lhsT=nchunk[buf][:, t, :], rhs=w4[:, :], start=True, stop=True,
                              skip_group_check=True)
                last.then_inc(s_nfree[buf], 1)

            def gathered_rows(q, g, used):
                pe.wait_ge(t_rows[g], used * (16 * TILES) + 16 * TILES)
                for t in range(TILES):
                    b, at = t // TB, t % TB * P
                    last = mm(psA[q][b][:, at:at + P], lhsT=rowsT[g][:, t, :], rhs=ident16[:, :], start=False, stop=False,
                              skip_group_check=True)
                last.then_inc(t_rowsfree[g], 1)

            def feature_product(i, q, u, b, prev):
                if b == 0:
                    pe.wait_ge(t_cx[q], (u + 1) * (16 * len(XPARTS)))
                    if prev:
                        pe.wait_ge(t_ln, i * NB + PRIME)
                else:
                    pe.wait_ge(t_Cfree, i * NB + (b + PRIME))
                pe.sem_inc(s_own["pe"], 1)
                mm(psCV[D:2 * D, 0:BLK], lhsT=wqx[:, :], rhs=cx[q][:, b * BLK:(b + 1) * BLK],
                   start=True, stop=True).then_inc(t_C, 1)

            def variances(i, b):
                pe.wait_ge(t_sq, i * NB + (b + 1))
                if b == 0:
                    pe.wait_ge(t_Cfree, i * NB + (NB + PRIME))
                else:
                    pe.wait_ge(t_ln, i * NB + (b + PRIME))
                mm(psCV[:, 0:BLK], lhsT=blockones[:, :], rhs=SQ[b][:, :], start=True, stop=True).then_inc(t_V, 1)

            def last_product(i, b):
                pe.wait_ge(t_R, i * NB + (b + 1 + PRIME))
                pe.wait_ge(t_zb, i * NB + (b + PRIME))
                for t in range(TB):
                    last = mm(psZ[0:P, t * (D + 1):(t + 1) * (D + 1)], lhsT=R[b][:, t * P:(t + 1) * P], rhs=wm[:, :],
                              start=True, stop=True, skip_group_check=True)
                last.then_inc(t_Z, 1)

            def body(i, q, u, cats=(), prev=True, graph=None, project=None, nodes=None, last=False):
                if not prev:
                    pass_start(0)
                count = NKT - skipped(cats)
                for v, kt, c, j in one_hot_steps(cats):
                    if kt is not None:
                        pe.wait_ge(t_oh, i * NKT + (kt + 1))
                        for b in range(NB):
                            if kt == 0:
                                pe.wait_ge(t_Afree, i * NB + (b + 1))
                            ins = mm(psA[q][b][:, 0:BLK], lhsT=T16[:, j, c, :], rhs=onehot[kt % RING][:, b * BLK:(b + 1) * BLK],
                                     start=kt == 0, stop=kt == count - 1, skip_group_check=True)
                            if kt == count - 1 and b == 0:
                                ins.then_inc(t_A, 1)
                        ins.then_inc(t_ohfree, 1 if kt else 1 + skipped(cats))
                    for g, used in cats:
                        if v == AT_CATS[g]:
                            gathered_rows(q, g, used)
                    if project and v in AT_NODES:
                        project_nodes(project, graph[1], AT_NODES.index(v))
                    if graph and v in AT_TILE:
                        graph_tile(graph[0], graph[1], AT_TILE.index(v))
                    if prev and v in AT_PE["variance"]:
                        variances(i - 1, AT_PE["variance"].index(v))
                    if v in AT_PE["feature"]:
                        feature_product(i, q, u, AT_PE["feature"].index(v), prev)
                    if prev and v in AT_PE["product"]:
                        last_product(i - 1, AT_PE["product"].index(v))

            def between(n):
                count = rounds if n else deg_rounds
                with pe.If(count > RSN[n]):
                    with pe.Fori(RSN[n], count) as r:
                        for t in range(ROUND):
                            graph_tile(n, r, t)
                for c in range(2 if n else 1):
                    ins = zero_product(c, False)
                ins.then_inc(s_pass, 1)
                if n + 1 < len(passes):
                    pass_start(n + 1)

            schedule(pe, body, between)
            for b in range(NB):
                variances(NSB - 1, b)
            for b in range(NB):
                last_product(NSB - 1, b)

        @block.scalar
        def _(act):
            A = nc.scalar.activation
            act.dma_start(ends[:, 0, :], src_e).then_inc(s_ends, 16)
            act.dma_start(ends[:, 1, :], dst_e).then_inc(s_ends, 16)
            act.wait_ge(s_w4, 1)
            for k in range(2):
                for c in range(2):
                    act.dma_start(w4[D * k:D * k + D, 2 * k + c:2 * k + c + 1],
                                  Wf[c * D:(c + 1) * D].rearrange("(d o) -> d o", o=1)).then_inc(s_w4, 16)
            act.wait_ge(s_cont, 16)
            for k in range(2):
                for f in range(CONT):
                    if k:
                        act.wait_ge(s_bsq, f + 1)
                    if k or f:
                        act.wait_ge(s_sqs, k * CONT + f)
                    A(sqj[:, :], cont_f[:, f, :], (ACT.Copy, ACT.Square)[k], accum_out=bstat[:, k, f:f + 1]).then_inc(s_sqs, 1)
            act.wait_ge(s_bv, 1)
            A(bstat[:, 3, :], bstat[:, 2, :], ACT.Sqrt).then_inc(s_bv, 1)
            nc.scalar.preload_act_table_set("natural_log_exp_and_others")
            act.wait_ge(s_nr, 1)
            rounds = act.value_load(nround[0:1, 1:2], min_val=RS, max_val=ROUNDS_MAX)
            act.wait_ge(s_prep, 1)

            def feature_evac(i, q, b, prev=True):
                act.wait_ge(t_C, i * NB + (b + 1))
                if prev:
                    act.wait_ge(t_xn, (i - 1) * NB + PRIME)
                A(X[q][b][D:2 * D, :], psCV[D:2 * D, 0:BLK], ACT.Identity, bias=bqc[D:2 * D, :]).then_inc(t_Cfree, 1)

            def lo_copy(i, q, b):
                if b == 0:
                    act.wait_ge(t_A, i + 1)
                else:
                    act.wait_ge(t_ohfree, i * NKT + (NKT + RING))
                act.wait_ge(t_x, i * NB + PRIME)
                A(lo_part[b], psA[q][b][D:2 * D, 0:BLK], ACT.Copy, scale=sc_i[0:D, 0:1].bitcast(f32)).then_inc(t_lo, 1)

            def square(i, q, b):
                act.wait_ge(t_x, i * NB + (b + 1 + PRIME))
                act.wait_ge(t_Cfree, i * NB + (b + 1 + PRIME))
                act.wait_ge(t_V, i * NB + PRIME)
                A(SQ[b][:, :], X[q][b][:, :], ACT.Square).then_inc(t_sq, 1)

            def rstd(i, b):
                act.wait_ge(t_V, i * NB + (b + 1 + PRIME))
                act.wait_ge(t_R, i * NB + PRIME)
                A(SD[b], psCV[:, 0:BLK], ACT.Ln, bias=eps[:, :]).then_inc(t_ln, 1)
                act.wait_ge(t_ln, i * NB + (b + 1 + PRIME))
                A(SD[b], SD[b], ACT.Exp, scale=-0.5).then_inc(t_sd, 1)

            def relu(i, b):
                act.wait_ge(t_xn, i * NB + (b + 1 + PRIME))
                act.wait_ge(t_Z, i * NB + PRIME)
                A(R[b], SD[b], ACT.Relu, scale=g12[:, :], bias=b12[:, :]).then_inc(t_R, 1)

            def last_square(i, b):
                act.wait_ge(t_zb, i * NB + (b + 1 + PRIME))
                act.wait_ge(t_red, i * NB + PRIME)
                A(ZQ[b][:, :, :], ZB[b][:, :, 0:D], ACT.Square).then_inc(t_zq, 1)

            def graph_tile(n, r, t):
                k = passes[n]
                h = t // TOP
                if t % TOP == 0:
                    act.wait_ge(s_gath[k][h], r * (16 * TOP) + 16 * TOP)
                    act.wait_ge(s_lo8[k], 2 * r + (h + 1))
                act.wait_ge(s_ohu[k], r * ROUND + (t + 1 + GRH - GR))
                for v in range(4):
                    ins = A(oh_lo[t % GR][:, v, :], oh_lo8[h][:, t % TOP, :], ACT.Copy, scale=gath[h][:, t % TOP, v:v + 1])
                ins.then_inc(s_lo[k], 1)

            def load_nodes(project, r, s):
                buf, used = node_step(project, s)
                act.wait_ge(s_nfree[buf], used + PRIME)
                act.sem_inc(s_own["act"], 1)
                act.dma_start(nchunk[buf], node_emb[:, ds(r * (len(AT_NODES) * NPAIR * P) + s * (NPAIR * P), NPAIR * P)].rearrange(
                    "k (h p) -> k h p", p=P)).then_inc(s_nch[buf], 16)

            def body(i, q, u, cats=(), prev=True, graph=None, project=None, nodes=None, last=False):
                if not prev:
                    feature_evac(i, q, 0, False)
                    feature_evac(i, q, 1, False)
                    return
                j, p = i - 1, 1 - q
                step = dict(lo=lambda b: lo_copy(j, p, b), square=lambda b: square(j, p, b), rstd=lambda b: rstd(j, b),
                            relu=lambda b: relu(j, b), feature=lambda b: feature_evac(i, q, b), zsquare=lambda b: last_square(j, b))
                for kt in range(NKT):
                    for what, at in AT_ACT.items():
                        if kt in at:
                            step[what](at.index(kt))
                    if project and kt in AT_NODES_LOAD:
                        load_nodes(project, graph[1], AT_NODES_LOAD.index(kt))
                    if graph and graph[0]:
                        for t in range(ROUND):
                            if max(AT_TILE[t] - ACT_LEAD, 0) == kt:
                                graph_tile(graph[0], graph[1], t)
                    if nodes == 0 and kt == 8:
                        act.wait_ge(s_degm, 1)
                        A(degm[:, :], degm[:, :], ACT.Sqrt).then_inc(s_degs, 1)
                        nc.scalar.preload_act_table_set("natural_log_exp_and_others")

            def between(n):
                if n:
                    with act.If(rounds > RS):
                        with act.Fori(RS, rounds) as r:
                            for t in range(ROUND):
                                graph_tile(n, r, t)

            schedule(act, body, between)
            i, q = NSB - 1, (NSB - 1) % 2
            for step in (lambda b: lo_copy(i, q, b), lambda b: square(i, q, b), lambda b: rstd(i, b), lambda b: relu(i, b),
                         lambda b: last_square(i, b)):
                for b in range(NB):
                    step(b)
            act.wait_ge(s_fin, 1)
            A(var3[:, :], var3[:, :], ACT.Ln, scale=1.0 / D, bias=eps[0:P, :]).then_inc(s_fs, 1)
            act.wait_ge(s_fs, 1)
            A(var3[:, :], var3[:, :], ACT.Exp, scale=-0.5).then_inc(s_fs, 1)

        @block.vector
        def _(dve):
            V = nc.vector
            chain = [0]

            def link(ins):
                chain[0] += 1
                ins.then_inc(s_dve, 1)
                dve.wait_ge(s_dve, chain[0])

            V.memset(w4[:, :], 0.0).then_inc(s_w4, 1)
            V.memset(onesm[:, :], 1.0)
            for x in primed:
                dve.sem_inc(x, PRIME)
            dve.sem_inc(t_ohfree, RING)
            dve.sem_inc(t_Afree, 2 * NB)
            for k in passes:
                dve.sem_inc(s_ohu[k], GRH)
                dve.sem_inc(s_hi[k], PRIME)
            for k in passes[1:]:
                dve.sem_inc(s_lo[k], BACK)

            def centre(w, parts, n):
                m = wsum[0:parts, 0:1]
                link(V.tensor_reduce(m, w, AX.X, ALU.add))
                link(V.tensor_scalar(m, m, 1.0 / n, None, ALU.mult))
                link(V.tensor_scalar(w, w, m, None, ALU.subtract))

            def power_scale(bits, top):
                link(V.tensor_scalar(bits[:, 0:1], top.bitcast(i32), 0x7F800000, None, ALU.bitwise_and))
                link(V.tensor_scalar(bits[:, 0:1], bits[:, 0:1], -float(F_MAX * 2 ** 23), float(2 ** 23), ALU.add, ALU.max))
                link(V.tensor_scalar(bits[:, 1:2], bits[:, 0:1], -1.0, 254.0 * 2 ** 23, ALU.mult, ALU.add))

            dve.wait_ge(s_first, 32)
            m5 = wsum[0:D, 0:CATE]
            link(V.tensor_reduce(m5, wc[:, :, :], AX.X, ALU.add))
            link(V.tensor_scalar(m5, m5, 1.0 / D, None, ALU.mult))
            link(V.tensor_tensor(wc[:, :, :], wc[:, :, :],
                                 m5.rearrange("p (c o) -> p c o", o=1).broadcast_to([D, CATE, D]), ALU.subtract))
            dve.sem_inc(s_wc, 1)
            centre(bcb[:, :], P, D)
            link(V.memset(tmax[:, :], 0.0))
            for j in range(KT):
                dve.wait_ge(s_tps, j + 1)
                V.tensor_copy(Tf[:, j, :, :], psT[j % 2][0:P, 0:CATE * D].rearrange("p (c d) -> p c d", c=CATE)).then_inc(s_tev, 1)
            dve.wait_ge(s_tev, KT)
            link(V.memset(Tf[0:1, 0, :, :], 0.0))
            link(V.tensor_tensor(Tf[:, :, 0, :], Tf[:, :, 0, :],
                                 bcb[:, :].rearrange("p (o d) -> p o d", o=1).broadcast_to([P, KT, D]), ALU.add))
            V.tensor_reduce(tmax[0:P, 0:1], Tf, AX.XYZ, ALU.max, apply_absolute_value=True).then_inc(s_tmax, 1)
            dve.wait_ge(s_par, 16 * NPAR)
            V.memset(one1[:, :], 1.0)
            centre(bqr[:, :], 1, D)
            dve.sem_inc(s_bqp, 1)

            dve.wait_ge(s_sqs, CONT)
            dve.sem_inc(s_bs, 1)
            dve.wait_ge(s_bt, 1)
            link(V.tensor_scalar(bstat[:, 0, :], psS[0:P, 0:CONT], 1.0 / E, None, ALU.mult))
            for c in range(CONT):
                V.tensor_scalar(cont_f[:, c, :], cont_f[:, c, :], bstat[:, 0, c:c + 1], None, ALU.subtract).then_inc(s_bsq, 1)

            dve.wait_ge(s_tall, 1)
            power_scale(sc_i, tmax[:, 1:2])
            Tv = Tf.rearrange("p j c d -> p (j c) d")
            T16v = T16[:, :, :, :].rearrange("p j c d -> p (j c) d")
            link(V.tensor_scalar(Tv, Tv, sc_i[0:P, 1:2].bitcast(f32), None, ALU.mult))
            link(V.tensor_copy(T16v[:, :, 0:D], Tv))
            link(V.tensor_tensor(T16v[:, :, D:2 * D], Tv, T16v[:, :, 0:D], ALU.subtract))
            dve.sem_inc(s_t16, 1)
            dve.wait_ge(s_id, 2)
            V.tensor_copy(ident16[:, :], ident[:, :])
            dve.wait_ge(s_iota, 3)
            V.tensor_copy(pidx[:, :], pidx_i[:, :])
            V.tensor_copy(iota16[:, :], iota_i[:, 0, :])
            V.tensor_copy(ebase[:, :], ebase_i[:, :])
            link(V.memset(zero_l[:, :], 0.0))
            dve.sem_inc(s_ready, 1)
            link(V.tensor_scalar(col_key, iota_i[:, :, :], -256.0, 65536.0, ALU.add, ALU.mult))
            dve.wait_ge(s_ends, 32)
            link(V.tensor_copy(dst_f, ends[:, 1, :]))
            link(V.tensor_scalar(valid, dst_f, float(N), None, ALU.is_lt))
            link(V.tensor_reduce(cnt[:, :], valid.rearrange("p (h c) -> p h c", h=2), AX.X, ALU.add))
            link(V.tensor_scalar(cleft[:, :], cnt[:, :], -float(TOP * (RS - 1)), 0.0, ALU.add, ALU.max))
            link(V.tensor_reduce(cmax[:, 1:2], cleft[:, :], AX.X, ALU.add))
            V.tensor_reduce(cmax[:, 0:1], cnt[:, :], AX.X, ALU.max).then_inc(s_cmax, 1)
            flat = "p h c -> p (h c)"
            dve.wait_ge(s_keyfill, 1)
            link(V.tensor_tensor(dst_f, dst_f, col_key.rearrange(flat), ALU.add))
            link(V.copy_predicated(keys[:, 1, :, :].rearrange(flat), valid, dst_f))
            link(V.tensor_tensor(dst_f, ends[:, 0, :], col_key.rearrange(flat), ALU.add))
            link(V.copy_predicated(keys[:, 0, :, :].rearrange(flat), valid, dst_f))
            dve.wait_ge(s_call, 1)
            link(V.tensor_scalar(nround[:, 2:3], call[:, 0:1], float(TOP - 1), float(TOP), ALU.add, ALU.max))
            link(V.tensor_scalar(nround[:, 0:1], nround[:, 2:3], 3, None, ALU.arith_shift_right))
            link(V.tensor_scalar(mergeable[:, :], call[:, 1:2].broadcast_to([P, ROUND]), float(ROUND), None, ALU.is_le))
            link(V.tensor_scalar(flag[:, :], call[:, 1:2], float(ROUND), None, ALU.is_gt))
            link(V.tensor_scalar(nround[:, 1:2], nround[:, 0:1], -float(RS), flag[:, 0:1], ALU.add, ALU.mult))
            V.tensor_scalar(nround[:, 1:2], nround[:, 1:2], float(RS), None, ALU.add).then_inc(s_nr, 1)
            dve.wait_ge(s_nr, 1)
            deg_rounds = dve.value_load(nround[0:1, 0:1], min_val=1, max_val=ROUNDS_MAX)
            rounds = dve.value_load(nround[0:1, 1:2], min_val=RS, max_val=ROUNDS_MAX)

            dve.wait_ge(s_sqs, 2 * CONT)
            dve.sem_inc(s_bs, 1)
            dve.wait_ge(s_bt, 2)
            V.tensor_scalar(bstat[:, 2, :], psS[0:P, 8:8 + CONT], 1.0 / E, EPS, ALU.mult, ALU.add).then_inc(s_bv, 1)
            dve.wait_ge(s_bv, 2)
            link(V.reciprocal(bstat[:, 3, :], bstat[:, 3, :]))
            link(V.tensor_tensor(bnp[:, 0, :], bnp[:, 0, :], bstat[:, 3, :], ALU.mult))
            for c in range(CONT):
                ins = V.tensor_scalar(cont_f[:, c, :], cont_f[:, c, :], bnp[:, 0, c:c + 1], bnp[:, 1, c:c + 1], ALU.mult, ALU.add)
            link(ins)
            link(V.tensor_copy(cont_part, cont_f))
            dve.sem_inc(s_cxp, 1)

            link(V.tensor_tensor(cont_f, cont_f, cont_part, ALU.subtract))
            dve.wait_ge(s_store, 32)
            link(V.tensor_copy(cont_part, cont_f))
            dve.sem_inc(s_cxp, 1)
            centre(wm[:, 0:D], 128, D)
            centre(wq6[:, :], XROWS, D)
            link(V.tensor_copy(wqp[:, 0, :], wq6[:, :]))
            link(V.tensor_tensor(wq6[:, :], wq6[:, :], wqp[:, 0, :], ALU.subtract))
            link(V.tensor_copy(wqp[:, 1, :], wq6[:, :]))
            link(V.tensor_tensor(wqp[:, 2, :], wq6[:, :], wqp[:, 1, :], ALU.subtract))
            link(V.tensor_scalar(wqr[:, :], wqp[:, 0, :], pmask[:, 0:1], None, ALU.mult))
            link(V.scalar_tensor_tensor(wqr[:, :], wqp[:, 1, :], pmask[:, 1:2], wqr[:, :], ALU.mult, ALU.add))
            link(V.scalar_tensor_tensor(wqx[:, :], wqp[:, 2, :], pmask[:, 2:3], wqr[:, :], ALU.mult, ALU.add))
            V.memset(eps[:, :], EPS)
            link(V.memset(blockones[:, :], 0.0))
            for k in range(2):
                V.memset(blockones[k * D:(k + 1) * D, k * D:(k + 1) * D], 1.0 / D)

            link(V.tensor_tensor(cont_f, cont_f, cont_part, ALU.subtract))
            dve.wait_ge(s_store, 48)
            link(V.tensor_copy(cont_part, cont_f))
            dve.sem_inc(s_cxp, 1)
            link(V.tensor_tensor(gw[:, :], v3[:, 0, :], v3[:, 2, :], ALU.mult))
            link(V.tensor_tensor(wtmp[:, :], wm[:, 0:D], gw[:, :], ALU.mult))
            link(V.tensor_reduce(wm[:, D:D + 1], wtmp[:, :], AX.X, ALU.add))
            link(V.tensor_copy(brow[:, 0:D], v3[0:P, 3, :]))
            centre(brow[:, 0:D], P, D)
            link(V.tensor_tensor(wtmp[0:P, :], brow[:, 0:D], gw[0:P, :], ALU.mult))
            link(V.tensor_reduce(brow[:, D:D + 1], wtmp[0:P, :], AX.X, ALU.add))
            link(V.tensor_tensor(wtmp[0:P, :], v3[0:P, 1, :], v3[0:P, 2, :], ALU.mult))
            link(V.tensor_reduce(k0[:, 0:1], wtmp[0:P, :], AX.X, ALU.add))
            link(V.tensor_tensor(k0[:, 1:2], k0[:, 0:1], bfb[:, :], ALU.add))
            dve.wait_ge(s_bqd, 1)
            V.tensor_copy(bqc[D:2 * D, :], psB[D:2 * D, 0:1])

            dve.sem_inc(s_prep, 1)

            PACK_STEPS = 23
            MAGIC = 1.5 * 2 ** 23

            def pack_steps(r):
                n = [0]
                steps = []

                def step(make, count=1, own=False):
                    before = n[0]
                    n[0] += count

                    def run():
                        dve.wait_ge(s_ext, r * PACK_STEPS + (before + PRIME))
                        if own:
                            dve.sem_inc(s_own["dve"], 1)
                        make()
                    steps.append(run)

                def plain(make):
                    step(lambda: make().then_inc(s_ext, 1))

                pairs4 = [(a, h) for a in range(2) for h in range(2)]
                for k, (a, h) in enumerate(pairs4):
                    step(lambda a=a, h=h: V.max(top8[:, a, h, :], keys[:, a, h, :]).then_inc(s_ext, 1), own=True)
                plain(lambda: V.tensor_copy(pk[:, :, :], top8[:, :, :, :].rearrange("p a h t -> p a (h t)")))
                for a, h in pairs4:
                    step(lambda a=a, h=h: V.match_replace(keys[:, a, h, :], top8[:, a, h, :], keys[:, a, h, :], (FILL_SRC, FILL_DST)[a]).then_inc(s_ext, 1), own=True)
                plain(lambda: V.tensor_copy(pk_i[:, :, :], pk[:, :, :]))
                plain(lambda: V.tensor_scalar(pk_c[:, :], pk_i[:, 1, :], 16, None, ALU.arith_shift_right))
                plain(lambda: V.tensor_scalar(pk_i[:, :, :], pk_i[:, :, :], 0xFFFF, None, ALU.bitwise_and))
                plain(lambda: V.tensor_copy(rnd[:, 0, :], pk_i[:, 0, :]))
                plain(lambda: V.tensor_scalar(pk_f[:, 1, :], pk_c[:, :], -256.0, float(2 ** 18), ALU.is_lt, ALU.mult))
                plain(lambda: V.tensor_tensor(pk_f[:, 0, :], ebase[:, :], pk_c[:, :], ALU.add))
                plain(lambda: V.tensor_tensor(rnd[:, 2, :], pk_f[:, 0, :], pk_f[:, 1, :], ALU.add))
                pdst, plo, phi = pk_f[:, 0, :], rnd[:, 3, :].bitcast(f32), rnd[:, 4, :].bitcast(f32)
                plain(lambda: V.tensor_copy(pdst, pk_i[:, 1, :]))
                plain(lambda: V.tensor_scalar(rnd[:, 1, :], pdst, float(N - 1), None, ALU.min))
                plain(lambda: V.tensor_scalar(plo, pdst, -(HI - 1) / 2, 1.0 / HI, ALU.add, ALU.mult))
                plain(lambda: V.tensor_scalar(plo, plo, MAGIC, None, ALU.add))
                plain(lambda: V.tensor_scalar(plo, plo, MAGIC, None, ALU.subtract))
                plain(lambda: V.scalar_tensor_tensor(phi, plo, -float(HI), pdst, ALU.mult, ALU.add))
                plain(lambda: V.tensor_copy(packed[:, :, ds(r * ROUND, ROUND)], rnd[:, :, :]))
                assert n[0] == PACK_STEPS, n[0]
                return steps

            def graph_half(n, r, h):
                k = passes[n]
                dve.wait_ge(s_hi[k], r * ROUND + (h * TOP + PRIME))
                if n == 0:
                    dve.wait_ge(s_ext, r * PACK_STEPS + (PACK_STEPS + PRIME))
                V.tensor_copy(slotd[h][:, :, :], packed[:, 3:5, ds(r * ROUND + h * TOP, TOP)]).then_inc(s_slotd[k], 1)
                dve.wait_ge(s_slotd[k], 2 * r + (h + 1))
                if n:
                    dve.wait_ge(s_lo[k], r * ROUND + (h * TOP + PRIME))
                V.tensor_tensor(oh_lo8[h][:, :, :],
                                iota16[:, 0:P].rearrange("p (o c) -> p o c", o=1).broadcast_to([P, TOP, P]),
                                slotd[h][:, 0, :].bitcast(f32).rearrange("p (t o) -> p t o", o=1).broadcast_to([P, TOP, P]),
                                ALU.is_equal).then_inc(s_lo8[k], 1)

            def graph_tile(n, r, t):
                k = passes[n]
                h = t // TOP
                if t % TOP == 0:
                    graph_half(n, r, h)
                    if n == 0:
                        dve.wait_ge(s_lo8[k], 2 * r + (h + 1))
                dve.wait_ge(s_ohu[k], r * ROUND + (t + 1))
                V.tensor_scalar(oh_hi[t % GRH][:, :], iota16[:, :], slotd[h][:, 1, t % TOP:t % TOP + 1].bitcast(f32), None,
                                ALU.is_equal).then_inc(s_hi[k], 1)

            def second_ends():
                for a in range(2):
                    at = (RS - 1 + a) * ROUND
                    V.tensor_scalar(isfirst[:, a * TOP:(a + 1) * TOP], packed[:, 2, at:at + TOP], float(E), None, ALU.is_lt)
                for j in range(ROUND):
                    back = ROUND - 1 - j
                    at = (RS - 1 + back // TOP) * ROUND + TOP + back % TOP
                    ins = V.tensor_copy(merged[:, :, j:j + 1], packed[:, :, at:at + 1])
                link(ins)

            def merge(f0, f1):
                if f0 == 0:
                    for f in range(5):
                        for a in range(2):
                            at = (RS - 1 + a) * ROUND
                            ins = V.copy_predicated(merged[:, f, a * TOP:(a + 1) * TOP], isfirst[:, a * TOP:(a + 1) * TOP], packed[:, f, at:at + TOP])
                    link(ins)
                for f in range(f0, f1):
                    ins = V.copy_predicated(packed[:, f, (RS - 1) * ROUND:RS * ROUND], mergeable[:, :], merged[:, f, :])
                link(ins)

            def node_steps(n):
                both = lambda x: x[:, :].rearrange("p (o h) -> p o h", o=1).broadcast_to([P, 2, HI])
                steps = []
                add = steps.append

                def first():
                    dve.wait_ge(s_pass, n + 1)
                    if n == 0:
                        V.tensor_scalar(degm[:, :], acc[0][0:P, 0:HI], 1.0, None, ALU.max).then_inc(s_degm, 1)
                        V.tensor_scalar(dis[:, :], acc[0][0:P, 0:HI], 0.0, None, ALU.is_gt).then_inc(s_accz, 1)
                    else:
                        for c in range(2):
                            ins = V.scalar_tensor_tensor(xl[:, c, :], acc[c][0:P, 0:HI], us_i[:, 0:1].bitcast(f32), dis[:, :],
                                                         ALU.mult, ALU.mult)
                        ins.then_inc(s_accz, 1)
                    dve.wait_ge(s_accz, n + 1)
                add(first)
                if n == 0:
                    add(lambda: dve.wait_ge(s_xev, RS_DEG // 2 * 2 + PRIME))
                    add(lambda: link(V.tensor_scalar(outn[:, :, :], xnode[:, :, :], 1.0 / (LAYERS + 1), None, ALU.mult)))
                    add(second_ends)
                    add(lambda: None)
                    add(lambda: merge(0, 2))
                    add(lambda: merge(2, 4))
                    add(lambda: merge(4, 5))
                    add(lambda: None)

                    def inverse():
                        dve.wait_ge(s_degs, 1)
                        link(V.reciprocal(degm[:, :], degm[:, :]))
                    add(inverse)
                    add(lambda: link(V.tensor_tensor(dis[:, :], dis[:, :], degm[:, :], ALU.mult)))
                else:
                    add(lambda: link(V.scalar_tensor_tensor(outn[:, :, :], xl[:, :, :], 1.0 / (LAYERS + 1), outn[:, :, :], ALU.mult, ALU.add)))
                src = xl if n else xnode
                if n < LAYERS:
                    add(lambda: link(V.tensor_tensor(un[:, :, :], src[:, :, :], both(dis), ALU.mult)))
                    add(lambda: V.tensor_reduce(umax[:, 0:1], un[:, :, :], AX.XY, ALU.max, apply_absolute_value=True).then_inc(s_umax, 1))
                    for _ in range(8):
                        add(lambda: None)

                    def scale():
                        dve.wait_ge(s_uall, n + 1)
                        power_scale(us_i, umax[:, 1:2])
                        if n:
                            dve.wait_ge(s_ust, 16 * n)
                    add(scale)
                    s = us_i[:, 1:2].bitcast(f32)
                    table = lambda part: utab[:, :, 2 * part:2 * part + 2].rearrange("p h a -> p a h")
                    add(lambda: link(V.tensor_scalar(part_h[:, :, :], un[:, :, :], s, None, ALU.mult)))
                    add(lambda: link(V.tensor_copy(table(0), part_h[:, :, :])))
                    add(lambda: link(V.scalar_tensor_tensor(part_h[:, :, :], un[:, :, :], s, part_h[:, :, :], ALU.mult, ALU.subtract)))
                    add(lambda: V.tensor_copy(table(1), part_h[:, :, :]).then_inc(s_utab, 1))
                else:
                    def out():
                        dve.wait_ge(s_ust, 16 * LAYERS)
                        V.tensor_copy(otab.rearrange("p h a -> p a h"), outn[:, :, :]).then_inc(s_outt, 1)
                    add(out)
                return steps

            def shift(q, count):
                dve.wait_ge(t_cate[q], count)
                V.tensor_scalar(cate_b[q], cate_b[q], pidx[:, 0:1], None, ALU.subtract).then_inc(t_cm, 1)

            def add_parts(i, q, b):
                dve.wait_ge(t_lo, i * NB + (b + 1))
                V.scalar_tensor_tensor(X[q][b][0:D, :], psA[q][b][0:D, 0:BLK], sc_i[0:D, 0:1].bitcast(f32),
                                       lo_part[b], ALU.mult, ALU.add).then_inc(t_x, 1)

            def free_bank(i, b):
                dve.wait_ge(t_x, i * NB + (b + 1 + PRIME))
                dve.sem_inc(t_Afree, 1)

            def normalise(i, q, b):
                dve.wait_ge(t_sd, i * NB + (b + 1 + PRIME))
                V.tensor_tensor(SD[b], X[q][b][:, :], SD[b], ALU.mult).then_inc(t_xn, 1)

            def last_bias(i, b):
                dve.wait_ge(t_Z, i * NB + (b + 1 + PRIME))
                dve.wait_ge(t_zq, i * NB + PRIME)
                V.tensor_tensor(ZB[b][:, :, :], psZ[0:P, 0:TB * (D + 1)].rearrange("p (t d) -> p t d", t=TB),
                                brow[:, :].rearrange("p (o d) -> p o d", o=1).broadcast_to([P, TB, D + 1]), ALU.add).then_inc(t_zb, 1)

            def last_numerator(i, b):
                dve.wait_ge(t_zb, i * NB + (b + 1 + PRIME))
                V.tensor_copy(num3[:, ds(i * TILES + b * TB, TB)], ZB[b][:, :, D])

            def last_variance(i, b):
                dve.wait_ge(t_zq, i * NB + (b + 1 + PRIME))
                V.tensor_reduce(var3[:, ds(i * TILES + b * TB, TB)], ZQ[b][:, :, :], AX.X, ALU.add).then_inc(t_red, 1)

            def copy_nodes(project, r):
                buf, used = node_step(project, len(AT_NODES) - 1)
                dve.wait_ge(s_nfree[buf], used + (1 + PRIME))
                w = len(AT_NODES) * NPAIR * 2
                V.tensor_copy(xnode[:, :, ds(r * w, w)], psO[0:P, 0:2 * w].rearrange("p (h a) -> p a h", a=2)).then_inc(s_xev, 1)

            def body(i, q, u, cats=(), prev=True, graph=None, project=None, nodes=None, last=False):
                if not prev:
                    shift(0, 16)
                packing = []
                if not prev or graph and graph[0] == 0:
                    packing = pack_steps(graph[1] + 1 if prev else 0)
                j, p = i - 1, 1 - q
                step = dict(parts=lambda b: add_parts(j, p, b), normalise=lambda b: normalise(j, p, b),
                            bias=lambda b: last_bias(j, b), zvariance=lambda b: last_variance(j, b))
                after = dict(parts=lambda b: free_bank(j, b), bias=lambda b: last_numerator(j, b))
                steps = node_steps(nodes) if nodes is not None else []
                dve.wait_ge(t_cm, i + 1)
                count = NKT - skipped(cats)
                for v, kt, c, jj in one_hot_steps(cats):
                    if kt is not None:
                        dve.wait_ge(t_ohfree, i * NKT + (kt + 1 + (skipped(cats) if kt >= RING else 0)))
                        V.tensor_scalar(onehot[kt % RING], cate_b[q][:, c, :], float(P * jj), None,
                                        ALU.is_equal).then_inc(t_oh, 1 if kt < count - 1 else 1 + skipped(cats))
                    for what, at in AT_DVE.items():
                        if prev and v in at:
                            step[what](at.index(v))
                        if prev and what in after and v - 1 in at:
                            after[what](at.index(v - 1))
                    if graph and v % 3 == 0 and v < 3 * ROUND:
                        graph_tile(graph[0], graph[1], v // 3)
                    if project and v == AT_NODES_COPY:
                        copy_nodes(project, graph[1])
                    if v % 2 and v // 2 < len(packing):
                        packing[v // 2]()
                    if v >= 5 and v - 5 < len(steps):
                        steps[v - 5]()
                    if v == 40 and not last:
                        shift(1 - q, (u + (2 if q else 1)) * 16)

            def between(n):
                count = rounds if n else deg_rounds
                with dve.If(count > RSN[n]):
                    with dve.Fori(RSN[n], count) as r:
                        for t in range(ROUND):
                            graph_tile(n, r, t)
                        if n == 0:
                            for step in pack_steps(r + 1):
                                step()

            schedule(dve, body, between)
            i, q = NSB - 1, (NSB - 1) % 2
            for step in (lambda b: add_parts(i, q, b), lambda b: normalise(i, q, b),
                         lambda b: (last_bias(i, b), last_numerator(i, b)), lambda b: last_variance(i, b)):
                for b in range(NB):
                    step(b)
            dve.wait_ge(t_red, NSB * NB + PRIME)
            dve.sem_inc(s_fin, 1)
            dve.wait_ge(s_ydl, 16)
            dve.wait_ge(s_sout, COLS // GSTEP)
            link(V.scalar_tensor_tensor(ys[:, :], yd[:, :], k0[:, 1:2], ys[:, :], ALU.add, ALU.add))
            dve.wait_ge(s_fs, 2)
            link(V.tensor_tensor(num3[:, :], num3[:, :], var3[:, :], ALU.mult))
            V.tensor_tensor(ys[:, :], ys[:, :], num3[:, :], ALU.add).then_inc(s_y, 1)


def kernel(**inputs):
    import numpy as _np
    import concourse.bacc as _bacc
    from concourse import mybir as _mybir
    from concourse.bass_utils import run_bass_kernel_spmd as _run

    a = {k.replace("L0_rec_", ""): _np.ascontiguousarray(v) for k, v in inputs.items()}
    edges = a["r_edge_index"]
    by_superblock = lambda x: _np.ascontiguousarray(
        x.reshape(x.shape[0], P, NSB, TILES).transpose(2, 0, 3, 1).reshape(NSB, -1))
    arrays = {
        "src": edges[0].reshape(P, COLS), "dst": edges[1].reshape(P, COLS),
        "cate": by_superblock(a["r_cate_features"]),
        "cate_tiles": _np.ascontiguousarray(
            a["r_cate_features"].reshape(CATE, P, NSB, TILES).transpose(2, 1, 0, 3).reshape(NSB, P, CATE * TILES)),
        "cont": by_superblock(a["cont_features"]),
        "node": _np.ascontiguousarray(a["node_emb"].reshape(P, HI // 2, 2, D).transpose(2, 3, 1, 0)).reshape(2 * D, HI // 2 * P),
        "tabT": _np.ascontiguousarray(a["cate_table"].T),
        "Wc": _np.ascontiguousarray(a["Wc"].reshape(CATE, D, D).transpose(1, 0, 2).reshape(D, CATE * D)),
        "bc": a["bc"], "ln1_g": a["ln1_g"], "ln1_b": a["ln1_b"], "bn_g": a["bn_g"], "bn_b": a["bn_b"],
        "Wq6": _np.ascontiguousarray(_np.broadcast_to(a["Wq"], (len(XPARTS), CONT, D)).reshape(XROWS, D)),
        "mask": _np.repeat(_np.eye(3, dtype=_np.float32)[[w for _, w in XPARTS]], CONT, axis=0),
        "bq": a["bq"], "ln2_g": a["ln2_g"], "ln2_b": a["ln2_b"], "Wm": a["Wm"], "bm": a["bm"],
        "ln3_g": a["ln3_g"], "ln3_b": a["ln3_b"], "Wf": a["Wf"].reshape(3 * D), "bf": a["bf"],
    }
    nc = _bacc.Bacc("TRN2", target_bir_lowering=False, num_devices=1)
    args = []
    for name, x in arrays.items():
        args.append(nc.dram_tensor(f"in_{name}", x.shape, _mybir.dt.from_np(x.dtype), kind="ExternalInput").ap())
    args.append(nc.dram_tensor("out_y", (P, COLS), _mybir.dt.float32, kind="ExternalOutput").ap())
    rec_kernel(nc, *args)
    r = _run(nc, [{f"in_{k}": v for k, v in arrays.items()}], core_ids=[0])
    return r.results[0]["out_y"].reshape(E)
```
